# Optimizing a Trainium2 kernel written in Bass

```python
import numpy as np
import jax
import jax.numpy as jnp

def _softmax(x, axis=-1):
    return jax.nn.softmax(x, axis=axis)

def _gelu(x):
    return jax.nn.gelu(x, approximate=True)

def _silu(x):
    return jax.nn.silu(x)

def _sigmoid(x):
    return jax.nn.sigmoid(x)

def _layernorm(x, axis=-1, eps=1e-05):
    m = jnp.mean(x, axis=axis, keepdims=True)
    v = jnp.var(x, axis=axis, keepdims=True)
    return (x - m) / jnp.sqrt(v + eps)

def _scatter_add(tgt, idx, src, axis=0):
    return tgt.at[idx].add(src)

def _segment_sum(src, seg, n):
    return jax.ops.segment_sum(src, seg, n)
kernel_name = 'mk_flamingo_gated_d1_seqx_r8_6fd95e'

def setup_inputs(seed: int=0):
    np.random.seed(seed)
    _w = jnp.asarray

    def _rec_inputs():
        import jax
        import jax.numpy as jnp
        _rk = jax.random.key(seed)
        x = -0.0003929 + 0.9999 * jax.random.normal(jax.random.fold_in(_rk, 1), (32, 56, 256), jnp.float32)
        _lenS = 56 - jax.random.randint(jax.random.fold_in(_rk, 7), (32,), 0, max(1, 56 // 4) + 1, jnp.int32)
        _lenS2 = 1500 - jax.random.randint(jax.random.fold_in(_rk, 8), (32,), 0, max(1, 1500 // 4) + 1, jnp.int32)
        _ctx_1024P = jax.random.normal(jax.random.fold_in(_rk, 11), (32, 16, 128), jnp.float32)
        _ctx_1024c = jax.random.dirichlet(jax.random.fold_in(_rk, 511), 0.3 * jnp.ones((16,), jnp.float32), (32, 1500))
        _ctx_1024t = jnp.einsum('bsk,bkd->bsd', _ctx_1024c, _ctx_1024P)
        _ctx_1024t = _ctx_1024t * jax.lax.rsqrt(jnp.mean(jnp.square(_ctx_1024t)) + 1e-12) * 0.953939
        ctx_1024 = -0.000494167 + 1.00018 * (_ctx_1024t + 0.3 * jax.random.normal(jax.random.fold_in(_rk, 611), (32, 1500, 128), jnp.float32))
        _validS = jnp.arange(56)[None, :] < _lenS[:, None]
        _validS2 = jnp.arange(1500)[None, :] < _lenS2[:, None]
        _causal = jnp.tril(jnp.ones((56, 56), dtype=bool))
        mask_BxS2_bf1 = jnp.ones((32, 1500), dtype=bool)
        _g = jax.random.normal(jax.random.fold_in(_rk, 9001), (2, 1), jnp.float32)
        _g = jnp.sign(_g) * jnp.maximum(jnp.abs(_g), 1.0) + (_g == 0) * 1.0
        g_xattn = _g[0]
        g_ffn = _g[1]
        return (x, ctx_1024, mask_BxS2_bf1, g_xattn, g_ffn)
    x, ctx_1024, mask_BxS2_bf1, g_xattn, g_ffn = _rec_inputs()

    def _L0_xattn_setup():
        import jax, jax.numpy as jnp
        import numpy as np
        N_HEADS = 16
        N_KV_HEADS = 8
        HEAD_DIM = 128
        D_TEXT = 256
        D_VISION = 128
        GROUPS = N_HEADS // N_KV_HEADS
        key = jax.random.key(seed)
        ks = jax.random.split(key, 6)
        B, T_text, T_vis = (4, 256, 72)
        text_hidden = jax.random.normal(ks[0], (B, T_text, D_TEXT), dtype=jnp.float32)
        vision_tokens = jax.random.normal(ks[1], (B, T_vis, D_VISION), dtype=jnp.float32)
        vision_mask = jnp.ones((B, T_vis), dtype=bool)
        s = 0.02
        Wq = jax.random.normal(ks[2], (D_TEXT, N_HEADS * HEAD_DIM), dtype=jnp.float32) * s
        Wk = jax.random.normal(ks[3], (D_VISION, N_KV_HEADS * HEAD_DIM), dtype=jnp.float32) * s
        Wv = jax.random.normal(ks[4], (D_VISION, N_KV_HEADS * HEAD_DIM), dtype=jnp.float32) * s
        Wo = jax.random.normal(ks[5], (N_HEADS * HEAD_DIM, D_TEXT), dtype=jnp.float32) * s
        return {'text_hidden': text_hidden, 'vision_tokens': vision_tokens, 'vision_mask': vision_mask, 'Wq': Wq, 'Wk': Wk, 'Wv': Wv, 'Wo': Wo}
    _L0_xattn_all = _L0_xattn_setup()
    _L0_xattn_in = {k: v for k, v in _L0_xattn_all.items() if k in ('Wq', 'Wk', 'Wv', 'Wo')}
    del _L0_xattn_all

    def _L0_ffn_setup():
        import jax, jax.numpy as jnp
        import numpy as np
        E = 8
        K = 2
        DIM = 256
        INTER = 176
        N_SHARED = 2
        STD = 0.02
        key = jax.random.key(seed)
        ks = jax.random.split(key, 9)
        B, S = (2, 256)
        return {'x': jax.random.normal(ks[0], (B, S, DIM), dtype=jnp.float32), 'gate_w': jax.random.normal(ks[1], (E, DIM), dtype=jnp.float32) * STD, 'router_bias': jnp.zeros((E,), dtype=jnp.float32), 'W1': jax.random.normal(ks[2], (E, DIM, INTER), dtype=jnp.float32) * STD, 'W3': jax.random.normal(ks[3], (E, DIM, INTER), dtype=jnp.float32) * STD, 'W2': jax.random.normal(ks[4], (E, INTER, DIM), dtype=jnp.float32) * STD, 'sw1': jax.random.normal(ks[5], (N_SHARED * INTER, DIM), dtype=jnp.float32) * STD, 'sw3': jax.random.normal(ks[6], (N_SHARED * INTER, DIM), dtype=jnp.float32) * STD, 'sw2': jax.random.normal(ks[7], (DIM, N_SHARED * INTER), dtype=jnp.float32) * STD}
    _L0_ffn_all = _L0_ffn_setup()
    _L0_ffn_in = {k: v for k, v in _L0_ffn_all.items() if k in ('gate_w', 'router_bias', 'W1', 'W3', 'W2', 'sw1', 'sw3', 'sw2')}
    del _L0_ffn_all
    return {'x': x, 'ctx_1024': ctx_1024, 'mask_BxS2_bf1': mask_BxS2_bf1, 'g_xattn': g_xattn, 'g_ffn': g_ffn, 'L0_xattn_Wq': _L0_xattn_in['Wq'], 'L0_xattn_Wk': _L0_xattn_in['Wk'], 'L0_xattn_Wv': _L0_xattn_in['Wv'], 'L0_xattn_Wo': _L0_xattn_in['Wo'], 'L0_ffn_gate_w': _L0_ffn_in['gate_w'], 'L0_ffn_router_bias': _L0_ffn_in['router_bias'], 'L0_ffn_W1': _L0_ffn_in['W1'], 'L0_ffn_W3': _L0_ffn_in['W3'], 'L0_ffn_W2': _L0_ffn_in['W2'], 'L0_ffn_sw1': _L0_ffn_in['sw1'], 'L0_ffn_sw3': _L0_ffn_in['sw3'], 'L0_ffn_sw2': _L0_ffn_in['sw2']}

def reference(x, ctx_1024, mask_BxS2_bf1, g_xattn, g_ffn, L0_xattn_Wq, L0_xattn_Wk, L0_xattn_Wv, L0_xattn_Wo, L0_ffn_gate_w, L0_ffn_router_bias, L0_ffn_W1, L0_ffn_W3, L0_ffn_W2, L0_ffn_sw1, L0_ffn_sw3, L0_ffn_sw2):
    import jax
    import jax.numpy as jnp

    def _L0_xattn_ref(text_hidden, vision_tokens, vision_mask, Wq, Wk, Wv, Wo):
        import jax, jax.numpy as jnp
        import numpy as np
        N_HEADS = 16
        N_KV_HEADS = 8
        HEAD_DIM = 128
        D_TEXT = 256
        D_VISION = 128
        GROUPS = N_HEADS // N_KV_HEADS
        B, T_text, _ = text_hidden.shape
        T_vis = vision_tokens.shape[1]
        scale = jnp.float32(np.sqrt(HEAD_DIM))
        q = (text_hidden @ Wq).reshape(B, T_text, N_HEADS, HEAD_DIM).transpose(0, 2, 1, 3)
        k = (vision_tokens @ Wk).reshape(B, T_vis, N_KV_HEADS, HEAD_DIM).transpose(0, 2, 1, 3)
        v = (vision_tokens @ Wv).reshape(B, T_vis, N_KV_HEADS, HEAD_DIM).transpose(0, 2, 1, 3)
        k = jnp.repeat(k, GROUPS, axis=1)
        v = jnp.repeat(v, GROUPS, axis=1)
        scores = jnp.einsum('bhtd,bhsd->bhts', q, k) / scale
        mask = vision_mask[:, None, None, :]
        scores = jnp.where(mask, scores, -jnp.inf)
        attn = jax.nn.softmax(scores, axis=-1)
        attn = jnp.nan_to_num(attn, nan=0.0)
        out = jnp.einsum('bhts,bhsd->bhtd', attn, v)
        out = out.transpose(0, 2, 1, 3).reshape(B, T_text, N_HEADS * HEAD_DIM)
        return out @ Wo

    def _L0_ffn_ref(x, gate_w, router_bias, W1, W3, W2, sw1, sw3, sw2):
        import jax, jax.numpy as jnp
        import numpy as np
        E = 8
        K = 2
        DIM = 256
        INTER = 176
        N_SHARED = 2
        STD = 0.02
        B, S, D = x.shape
        X = x.reshape(-1, D)
        T = X.shape[0]
        logits = jnp.einsum('td,ed->te', X, gate_w)
        scores = jax.nn.sigmoid(logits)
        sel = scores + router_bias[None, :]
        _, idx = jax.lax.top_k(sel, K)
        w = jnp.take_along_axis(scores, idx, axis=1)
        w = w / jnp.clip(jnp.sum(w, axis=-1, keepdims=True), 1e-12)
        gate_full = jnp.zeros((T, E), dtype=w.dtype).at[jnp.arange(T)[:, None], idx].set(w)
        h1 = jnp.einsum('td,edh->eth', X, W1)
        h3 = jnp.einsum('td,edh->eth', X, W3)
        y = jnp.einsum('eth,ehd->etd', jax.nn.silu(h1) * h3, W2)
        out = jnp.einsum('etd,te->td', y, gate_full)
        shared = jnp.einsum('th,dh->td', jax.nn.silu(jnp.einsum('td,hd->th', X, sw1)) * jnp.einsum('td,hd->th', X, sw3), sw2)
        out = out + shared
        return out.reshape(B, S, D)
    x = x + jnp.tanh(g_xattn[0]) * _L0_xattn_ref(_layernorm(x, axis=-1), ctx_1024, mask_BxS2_bf1, L0_xattn_Wq, L0_xattn_Wk, L0_xattn_Wv, L0_xattn_Wo)
    x = x + jnp.tanh(g_ffn[0]) * _L0_ffn_ref(_layernorm(x, axis=-1), L0_ffn_gate_w, L0_ffn_router_bias, L0_ffn_W1, L0_ffn_W3, L0_ffn_W2, L0_ffn_sw1, L0_ffn_sw3, L0_ffn_sw2)
    return x

_drawn_inputs = setup_inputs


def setup_inputs(seed=0):
    import zlib

    import numpy as np

    out = dict(_drawn_inputs(seed))
    spreads = {'L0_ffn_router_bias': (0.0, 0.8)}
    factors = {'L0_xattn_Wq': 8.0,
     'L0_xattn_Wk': 8.0,
     'L0_ffn_gate_w': 7.545,
     'L0_ffn_W1': 6.131,
     'L0_ffn_W3': 6.076,
     'L0_ffn_W2': 6.059,
     'L0_ffn_sw1': 3.061,
     'L0_ffn_sw3': 3.027,
     'L0_ffn_sw2': 3.028}
    for name, (base, spread) in spreads.items():
        noise = np.random.default_rng([zlib.crc32(name.encode()), seed]).standard_normal(out[name].shape)
        drawn = base * np.exp(spread * noise) if base else spread * noise
        out[name] = jnp.asarray(drawn.astype(out[name].dtype))
    for name, factor in factors.items():
        out[name] = (out[name] * factor).astype(out[name].dtype)
    return out
```

```python
from contextlib import ExitStack

import concourse.bass as bass
from concourse import mybir

F32, F16, BF16, U8 = mybir.dt.float32, mybir.dt.float16, mybir.dt.bfloat16, mybir.dt.uint8
ACT = mybir.ActivationFunctionType
ALU = mybir.AluOpType
AX = mybir.AxisListType

B, T, D = 32, 56, 256
S, DV = 1500, 128
H, KV, DH = 16, 8, 128
E, TOPK, INTER, NSH = 8, 2, 176, 352
NC = 12
SP = S // NC
Q = H * T
NQ = Q // 128
HALF = Q // 2
NSEG, SEG = 3, S // 3
GB = 8
G = B // GB
GT = GB * T
NT, TT = 4, GT // 4
KD = D // 128
HID = E * INTER + NSH
NH = -(-HID // 128)
HLAST = HID - (NH - 1) * 128
VC = DV + 1
EPS = 1e-5
MASKED = -1e30
WS = 64.0
NS = 256.0
LOW = 32
ROW = 64
NPB = 3

SEGS = [("seg", n) for n in range(NQ * NSEG)]
TURNS_NEXT = [(1, 1), (1, 1), (1, 1), (0, 1), (0, 1), (2, 1), (2, 1), (2, 1), (1, 1), (1, 1), (0, 0), (0, 0)]
M_AT, O_AT = 10, (3, 4)
N_M, N_O = NQ * NSEG + 1, 2


def turn_plan(has_next, has_last):
    plan, n = [], 0
    for k in range(NC):
        before, after = [], []
        if has_last and k in O_AT:
            before.append(("out", O_AT.index(k)))
        if has_next:
            for _ in range(TURNS_NEXT[k][0]):
                before.append(SEGS[n]); n += 1
            for _ in range(TURNS_NEXT[k][1]):
                after.append(SEGS[n]); n += 1
            if k == M_AT:
                before.append(("max", 0))
        plan.append((before, after))
    assert n == (len(SEGS) if has_next else 0)
    return plan


def build(nc, x, ctx, ctxT, mask, g_xattn, g_ffn, wqT, wkT, wvT, wo, gateT, rbias, w1, w3, w2, ident, blocks,
          expand, before, low, out):
    with ExitStack() as stack:
        def sb(name, shape, dt):
            return stack.enter_context(nc.sbuf_tensor(name, shape, dt))

        def ps(name, shape, dt):
            return stack.enter_context(nc.psum_tensor(name, shape, dt))

        def sem(name):
            return stack.enter_context(nc.semaphore(name))

        sc_ps = [ps(f"sc_ps{i}", [128, 2, 512], F32) for i in range(2)]
        o_ps = ps("o_ps", [128, 3, 512], F32)
        a_ps = ps("a_ps", [128, 512], F32)

        m_hl = [sb(f"m_{p}", [128, KD, H, 128], F16) for p in ("hi", "lo")]
        n_hl = [sb(f"n_{p}", [128, H, D], F16) for p in ("hi", "lo")]
        w1_hl = [sb(f"w1_{p}", [128, KD, NH * 128], F16) for p in ("hi", "lo")]
        w3_hl = [sb(f"w3_{p}", [128, KD, NH * 128], F16) for p in ("hi", "lo")]
        w2_hl = [sb(f"w2_{p}", [128, NH, D], F16) for p in ("hi", "lo")]
        gate_sb = sb("gate_sb", [128, KD, E], F32)
        bias_sb = sb("bias_sb", [128, E], F32)
        id_sb = sb("id_sb", [128, 128], F32)
        blocks_sb = sb("blocks_sb", [64, NQ, 128], BF16)
        expand_sb = sb("expand_sb", [128, NH * 128], F16)
        before_sb = sb("before_sb", [128, E * E], F32)
        gates_in = sb("gates_in", [128, 2], F32)
        gates_th = sb("gates_th", [128, 2], F32)
        gates = sb("gates", [128, 2], F32)
        nothing = sb("nothing", [128, 4], F32)
        low_rows = sb("low_rows", [64, 1], F32)

        q_all = sb("q_all", [128, GB, 2, Q], F16)
        q_st = sb("q_st", [128, 2, 2, Q], F16)

        c_f = sb("c_f", [128, NC, DV], F32)
        ct_f = sb("ct_f", [128, S], F32)
        mask_u8 = sb("mask_u8", [128, S], U8)
        keys = sb("keys", [128, 2, 2 * S + NC * (VC + DV)], F16)
        ct = [[keys[:, u, p * S:(p + 1) * S] for p in range(2)] for u in range(2)]
        cv = [keys[:, u, 2 * S:].rearrange("p (c n) -> p c n", c=NC) for u in range(2)]
        mask_b = sb("mask_b", [128, 2, S], BF16)
        shift_w = sb("shift_w", [128, 2, S], BF16)
        shift_m = sb("shift_m", [128, 2, Q], BF16)

        p_f = sb("p_f", [128, 2, Q], F32)
        p_hl = sb("p_hl", [128, NPB, 2, Q], F16)
        h_hl = p_hl
        s_f = p_f[:, 0, :].rearrange("p (u n) -> p u n", u=2)
        v_f = p_f[:, 1, :].rearrange("p (u n) -> p u n", u=2)
        max_junk = sb("max_junk", [128, SEG], BF16)
        maxes = sb("maxes", [128, NQ, NSEG], F32)
        neg_max = sb("neg_max", [128, NQ], F32)
        neg_pad = sb("neg_pad", [128, 128], F32)
        max_hi = sb("max_hi", [64, 128], BF16)
        max_rest = sb("max_rest", [64, 128], F32)
        den = sb("den", [128, NQ], F32)
        rden = sb("rden", [128, NQ], F32)
        o_f = sb("o_f", [128, NQ, DV], F32)

        xg = sb("xg", [128, NT, D], F32)
        xn = sb("xn", [128, NT, D], F32)
        xt_f = o_f[:, :, :].rearrange("p j d -> p (j d)").rearrange("p (k n) -> p k n", k=KD)
        xt_hl = [sb(f"xt_{p}", [128, KD, GT], F16) for p in ("hi", "lo")]
        proj_t = xt_f
        stats = sb("stats", [128, NT, 6], F32)
        mv = sb("mv", [128, NT, 2], F32)
        var_eps = sb("var_eps", [128, NT], F32)
        sd = sb("sd", [128, NT], F32)
        rstd = sb("rstd", [128, NT], F32)
        r_exp = sb("r_exp", [128, NT, E], F32)
        r_one = sb("r_one", [128, NT, E], F32)
        score = sb("score", [128, NT, E], F32)
        sel = sb("sel", [128, NT, E], F32)
        ahead, tied = [xn[:, a, :].rearrange("p (t e f) -> p t e f", t=NT, e=E) for a in range(2)]
        rank = sb("rank", [128, NT, E], F32)
        w_top = sb("w_top", [128, NT, E], F32)
        w_sum = sb("w_sum", [128, NT], F32)
        w_rec = sb("w_rec", [128, NT], F32)
        g_pad = sb("g_pad", [128, NT, 128], F32)
        g_hi = sb("g_hi", [64, GT], F16)
        g_t = sb("g_t", [128, GT], F16)

        consts_in = sem("consts_in")
        wq_in = sem("wq_in")
        wo_in = sem("wo_in")
        w13_in = sem("w13_in")
        w2_in = sem("w2_in")
        zeroed = sem("zeroed")
        zeroed_dve = sem("zeroed_dve")
        zeroed_w2 = sem("zeroed_w2")
        mix_made = sem("mix_made")
        mix_hi = sem("mix_hi")
        mix_used = sem("mix_used")
        w_hi = sem("w_hi")
        w_ready = sem("w_ready")
        th_ready = sem("th_ready")
        gates_ready = sem("gates_ready")

        ctx_in = sem("ctx_in")
        staged = [sem(f"staged{u}") for u in range(2)]
        row_in = [sem(f"row_in{u}") for u in range(2)]
        mask_ready = sem("mask_ready")
        ct_hi_ready = sem("ct_hi_ready")
        c_hi_ready = sem("c_hi_ready")
        split_done = sem("split_done")
        scored = sem("scored")
        p_hi_ready = sem("p_hi_ready")
        p_f_ready = sem("p_f_ready")
        p_ready = sem("p_ready")
        summed = sem("summed")
        a_full = sem("a_full")
        a_used = sem("a_used")
        neg_ready = sem("neg_ready")
        shift_ready = sem("shift_ready")
        o_ready = sem("o_ready")
        ot_hi = sem("ot_hi")
        dve_m = sem("dve_m")
        dve_o = sem("dve_o")

        x_in = sem("x_in")
        ln_step = sem("ln_step")
        ln_sd = sem("ln_sd")
        ln_rstd = sem("ln_rstd")
        xn_ready = sem("xn_ready")
        xt_full = sem("xt_full")
        xt_hi_ready = sem("xt_hi_ready")
        xt_ready = sem("xt_ready")
        q_full = sem("q_full")
        q_hi_ready = sem("q_hi_ready")
        q_ready = sem("q_ready")
        proj_full = sem("proj_full")
        proj_copied = sem("proj_copied")
        proj_back = sem("proj_back")
        x2_ready = sem("x2_ready")
        logits_full = sem("logits_full")
        r_exp_ready = sem("r_exp_ready")
        r_step = sem("r_step")
        gate_ready = sem("gate_ready")
        g_full = sem("g_full")
        g_ready = sem("g_ready")
        h_full = sem("h_full")
        silu_ready = sem("silu_ready")
        h_step = sem("h_step")
        h_ready = sem("h_ready")
        h_used = sem("h_used")
        y_ready = sem("y_ready")
        stored = sem("stored")

        room1 = q_all[:].rearrange("p b u q -> p (b u q)").bitcast(F32)
        room2 = keys[:].rearrange("p u n -> p (u n)").bitcast(F32)
        wq_f = room1[:, 0:H * D].rearrange("p (h n) -> p h n", h=H)
        wk_f = room1[:, H * D:H * D + KV * DV].rearrange("p (h n) -> p h n", h=KV)
        wo_f = room2[:, 0:H * D].rearrange("p (h n) -> p h n", h=H)
        wv_f = room2[:, H * D:H * D + KV * DV].rearrange("p (h n) -> p h n", h=KV)
        w1_f = room1[:, 0:KD * HID].rearrange("p (k n) -> p k n", k=KD)
        w3_f = room1[:, KD * HID:2 * KD * HID].rearrange("p (k n) -> p k n", k=KD)
        w2_f = room2[:, 0:NH * D].rearrange("p (t n) -> p t n", t=NH)
        banks = [sc_ps[0][:, 0, :], sc_ps[0][:, 1, :], sc_ps[1][:, 0, :], sc_ps[1][:, 1, :]]

        N_CONSTS = 9
        N_ZERO = 11
        N_MIX = 2 * H

        def mix_out(n):
            h = n % H
            return [(m_hl[p][:, :, h, :] if n < H else n_hl[p][:, h, :]) for p in range(2)], \
                (WS / DH ** 0.5 if n < H else NS)

        def mix_ps(n):
            b = banks[n % 4][:, 0:2 * 128]
            return b.rearrange("p (k n) -> p k n", k=KD) if n < H else b

        def turns_before(g, i):
            return g * ((N_M + N_O) * GB) + (i * (N_M + N_O) + (N_M if isinstance(i, int) and i == 0 else N_M - N_O))

        STEPS_M = 2

        def m_of(b):
            return b * STEPS_M

        def body_loop(eng, per_batch):
            def run(g):
                half = g * (GB // 2)
                per_batch(g, 0, 0, half, True, False)
                with eng.Fori(0, (GB - 2) // 2) as r:
                    per_batch(g, r * 2 + 1, 1, half + r, False, False)
                    per_batch(g, r * 2 + 2, 0, half + r + 1, False, False)
                per_batch(g, GB - 1, 1, half + (GB // 2 - 1), False, True)
            return run

        block = stack.enter_context(nc.Block())


        @block.sync
        def _(sp):
            for u in range(2):
                sp.sem_inc(row_in[u], 16)
            sp.sem_inc(stored, 16)
            sp.dma_start(wq_f, wqT.rearrange("h e n -> e h n")).then_inc(wq_in, 16)
            sp.dma_start(wk_f, wkT.rearrange("h e n -> e h n")).then_inc(wq_in, 16)
            sp.dma_start(wo_f, wo.rearrange("h e n -> e h n")).then_inc(wo_in, 16)
            sp.dma_start(wv_f, wvT.rearrange("h e n -> e h n")).then_inc(wo_in, 16)
            sp.dma_start(id_sb[:, :], ident).then_inc(consts_in, 16)
            sp.dma_start(blocks_sb[:, :, :], blocks).then_inc(consts_in, 16)
            sp.dma_start(expand_sb[:, :], expand).then_inc(consts_in, 16)
            sp.dma_start(before_sb[:, :], before).then_inc(consts_in, 16)
            sp.dma_start(gate_sb[:, :, :], gateT.rearrange("(k p) e -> p k e", k=KD)).then_inc(consts_in, 16)
            sp.dma_start(bias_sb[:, :], rbias.partition_broadcast(128)).then_inc(consts_in, 16)
            sp.dma_start(gates_in[:, 0:1], g_xattn.partition_broadcast(128)).then_inc(consts_in, 16)
            sp.dma_start(gates_in[:, 1:2], g_ffn.partition_broadcast(128)).then_inc(consts_in, 16)
            sp.dma_start(low_rows[:, :], low).then_inc(consts_in, 16)
            sp.wait_ge(mix_used, H)
            sp.dma_start(w1_f, w1.rearrange("(k p) n -> p k n", k=KD)).then_inc(w13_in, 16)
            sp.dma_start(w3_f, w3.rearrange("(k p) n -> p k n", k=KD)).then_inc(w13_in, 16)
            sp.wait_ge(mix_used, 2 * H)
            sp.dma_start(w2_f[:, 0:NH - 1, :], w2[0:(NH - 1) * 128, :].rearrange("(t p) n -> p t n", p=128)
                         ).then_inc(w2_in, 16)
            sp.dma_start(w2_f[0:HLAST, NH - 1, :], w2[(NH - 1) * 128:HID, :]).then_inc(w2_in, 16)

            def group(g):
                sp.dma_start(xg[0:TT, :, :], x[bass.ds(g * GT, GT), :].rearrange("(t p) n -> p t n", p=TT)
                             ).then_inc(x_in, 16)
            def batch(g, i, u, v, first, last):
                b = g * GB + i
                if not first:
                    sp.wait_ge(split_done, b * 2)
                sp.dma_start(c_f[0:SP, :, :], ctx[bass.ds(b, 1)].rearrange("b (p c) d -> (b p) c d", c=NC)
                             ).then_inc(ctx_in, 16)
                sp.dma_start(ct_f[:, :], ctxT[bass.ds(b, 1)].rearrange("b d s -> (b d) s")).then_inc(ctx_in, 16)
                sp.dma_start(mask_u8[:, :], mask[bass.ds(b, 1), :].rearrange("b s -> (b s)").partition_broadcast(128)
                             ).then_inc(ctx_in, 16)
                sp.wait_ge(q_ready, g * H + H)
                if not first:
                    sp.wait_ge(scored, b * NC - NC + 1)
                sp.dma_start(q_st[:, u, :, :], q_all[:, bass.ds(i, 1), :, :].rearrange("p b u q -> p (b u) q")
                             ).then_inc(staged[u], 16)
                sp.wait_ge(mask_ready, b + 1)
                sp.dma_start(shift_w[ROW:ROW + 1, u, :], mask_b[ROW:ROW + 1, u, :]).then_inc(row_in[u], 16)

            run = body_loop(sp, batch)
            with sp.Fori(0, G) as g:
                sp.wait_ge(stored, g * 16 + 16)
                group(g)
                run(g)
                sp.wait_ge(y_ready, (g + 1) * NT)
                sp.dma_start(out[bass.ds(g * GT, GT), :].rearrange("(t p) n -> p t n", p=TT), xg[0:TT, :, :]
                             ).then_inc(stored, 16)
            sp.wait_ge(stored, (G + 1) * 16)

        @block.gpsimd
        def _(pool):
            nc.gpsimd.memset(nothing[:, 0:1], 0.0)
            nc.gpsimd.memset(w1_hl[0][:, :, HID:], 0.0).then_inc(zeroed, 1)
            nc.gpsimd.memset(w1_hl[1][:, :, HID:], 0.0).then_inc(zeroed, 1)
            nc.gpsimd.memset(w3_hl[0][:, :, HID:], 0.0).then_inc(zeroed, 1)
            nc.gpsimd.memset(w3_hl[1][:, :, HID:], 0.0).then_inc(zeroed, 1)
            nc.gpsimd.memset(shift_w[:, :, :], 0.0).then_inc(zeroed, 1)
            nc.gpsimd.memset(shift_m[:, :, :], 0.0).then_inc(zeroed, 1)
            nc.gpsimd.memset(g_t[:, :], 0.0).then_inc(zeroed, 1)
            pool.wait_ge(zeroed, 7)
            nc.gpsimd.memset(shift_w[0:NQ, :, :], 1.0).then_inc(zeroed, 1)
            pool.wait_ge(zeroed, 8)
            nc.gpsimd.memset(shift_w[LOW:LOW + NQ, :, :], 1.0).then_inc(zeroed, 1)
            pool.wait_ge(zeroed, 9)
            nc.gpsimd.memset(shift_m[ROW:ROW + 1, :, :], 1.0).then_inc(zeroed, 1)
            pool.wait_ge(zeroed, 10)
            pool.wait_ge(w_ready, 3)
            for u in range(2):
                last = nc.gpsimd.memset(cv[u][:, :, DV:VC], 1.0)
            last.then_inc(zeroed, 1)
            pool.wait_ge(zeroed, N_ZERO)

            def batch(g, i, u, v, first, last):
                b = g * GB + i
                pool.wait_ge(ctx_in, b * 48 + 48)
                if not first:
                    pool.wait_ge(shift_ready, b)
                    pool.wait_ge(row_in[u], v * 16 + 16)
                nc.gpsimd.tensor_tensor(nothing[:, 0:1], nothing[:, 0:1], nothing[:, 0:1], ALU.add)
                nc.gpsimd.tensor_scalar(mask_b[:, u, :], mask_u8[:, :], -MASKED, MASKED, ALU.mult, ALU.add
                                        ).then_inc(mask_ready, 1)
                pool.wait_ge(ct_hi_ready, b + 1)
                nc.gpsimd.tensor_tensor(ct[u][1], ct_f[:, :], ct[u][0], ALU.subtract).then_inc(split_done, 1)
                pool.wait_ge(c_hi_ready, b + 1)
                nc.gpsimd.tensor_tensor(cv[u][0:SP, :, VC:], c_f[0:SP, :, :], cv[u][0:SP, :, 0:DV], ALU.subtract
                                        ).then_inc(split_done, 1)

            run = body_loop(pool, batch)
            with pool.Fori(0, G) as g:
                run(g)

        @block.scalar
        def _(act):
            act.wait_ge(consts_in, 16 * N_CONSTS)
            nc.scalar.activation(gates_th[:, :], gates_in[:, :], ACT.Tanh).then_inc(th_ready, 1)
            for n in range(N_MIX):
                (hi, _), scale = mix_out(n)
                act.wait_ge(mix_made, n + 1)
                nc.scalar.activation(hi, mix_ps(n), ACT.Copy, scale=scale).then_inc(mix_hi, 1)
            act.wait_ge(w13_in, 32)
            nc.scalar.activation(w1_hl[0][:, :, 0:HID], w1_f, ACT.Copy, scale=WS).then_inc(w_hi, 1)
            nc.scalar.activation(w3_hl[0][:, :, 0:HID], w3_f, ACT.Copy, scale=WS).then_inc(w_hi, 1)
            act.wait_ge(w2_in, 32)
            act.wait_ge(zeroed_w2, 1)
            nc.scalar.activation(w2_hl[0][:, :, :], w2_f, ACT.Copy, scale=WS).then_inc(w_hi, 1)

            def layer_norm(n):
                act.wait_ge(ln_step, n * 3 + 3)
                nc.scalar.activation(sd[0:TT, :], var_eps[0:TT, :], ACT.Sqrt).then_inc(ln_sd, 1)
                for k in range(KD):
                    act.wait_ge(xt_full, n * KD + k + 1)
                    nc.scalar.activation(xt_f[:, k, :], o_ps[:, k, 0:GT], ACT.Copy)
                    nc.scalar.activation(xt_hl[0][:, k, :], o_ps[:, k, 0:GT], ACT.Copy).then_inc(xt_hi_ready, 1)

            def split_ct(b, u, first):
                act.wait_ge(ctx_in, b * 48 + 48)
                if not first:
                    act.wait_ge(scored, b * NC - NC + 1)
                nc.scalar.activation(ct[u][0], ct_f[:, :], ACT.Copy).then_inc(ct_hi_ready, 1)

            def split_c(b, u, first):
                if not first:
                    act.wait_ge(summed, b * NC - NC)
                nc.scalar.activation(cv[u][0:SP, :, 0:DV], c_f[0:SP, :, :], ACT.Copy).then_inc(c_hi_ready, 1)

            def out_turn(b, j, i_last):
                lo, hi = (0, 512) if j == 0 else (512, Q)
                act.wait_ge(a_full, i_last)
                nc.scalar.activation(q_all[:, bass.ds(b[1], 1), 0, lo:hi].rearrange("p b q -> p (b q)"),
                                     a_ps[:, 0:hi - lo], ACT.Copy).then_inc(ot_hi, 1)

            def batch(g, i, u, v, first, last):
                b = g * GB + i
                plan = turn_plan(not last, not first)
                turn = 0
                base = turns_before(g, i)
                for k in range(NC):
                    n = b * NC + k
                    act.wait_ge(scored, n + 2)
                    if not (first and k < NPB):
                        act.wait_ge(summed, n - NPB + 1)
                    scores = sc_ps[k % 2][0:SP, :, 0:HALF]
                    nc.scalar.activation(p_hl[0:SP, k % NPB, 0, :].rearrange("p (a n) -> p a n", a=2), scores,
                                         ACT.Exp).then_inc(p_hi_ready, 1)
                    if not (first and k < 2):
                        act.wait_ge(p_ready, n - 1)
                    nc.scalar.activation(p_f[0:SP, k % 2, :].rearrange("p (a n) -> p a n", a=2), scores,
                                         ACT.Exp).then_inc(p_f_ready, 1)
                    if k == 0 and not last:
                        split_ct(b + 1, 1 - u, first)
                    if k == 3 and not last:
                        split_c(b + 1, 1 - u, first)
                    for kind, j in plan[k][0] + plan[k][1]:
                        turn += 1
                        if kind == "out":
                            out_turn((b, i - 1), j, base + turn)

            run = body_loop(act, batch)
            with act.Fori(0, G) as g:
                layer_norm(g * 2)
                for h in range(H):
                    act.wait_ge(q_full, g * H + h + 1)
                    nc.scalar.activation(q_all[:, :, 0, h * T:(h + 1) * T],
                                         banks[h % 4][:, 0:GT].rearrange("p (b t) -> p b t", b=GB), ACT.Copy,
                                         scale=1 / WS).then_inc(q_hi_ready, 1)
                b0 = g * GB
                split_ct(b0, 0, True)
                split_c(b0, 0, True)
                run(g)
                for j in range(N_O):
                    out_turn((b0 + GB - 1, GB - 1), j, g * ((N_M + N_O) * GB) + (N_M + N_O) * GB - N_O + j + 1)
                for k in range(KD):
                    act.wait_ge(proj_full, g * KD + k + 1)
                    nc.scalar.activation(proj_t[:, k, :], banks[k][:, 0:GT], ACT.Copy).then_inc(proj_copied, 1)
                layer_norm(g * 2 + 1)
                act.wait_ge(logits_full, g + 1)
                nc.scalar.activation(r_exp[0:TT, :, :].rearrange("p t e -> p (t e)"), a_ps[0:TT, 0:NT * E], ACT.Exp,
                                     scale=-1.0).then_inc(r_exp_ready, 1)
                for j in range(NH):
                    act.wait_ge(h_full, g * NH + j + 1)
                    if j >= 2:
                        act.wait_ge(h_step, (g * NH + j - 2) * 3 + 1)
                    nc.scalar.activation(s_f[:, j % 2, :], sc_ps[j % 2][:, 0, 0:GT], ACT.Silu, scale=1 / WS
                                         ).then_inc(silu_ready, 1)

        @block.vector
        def _(dve):
            dve.sem_inc(shift_ready, 1)
            nc.vector.memset(neg_pad[:, :], 0.0).then_inc(zeroed_dve, 1)
            nc.vector.memset(nothing[:, 1:3], 0.0)
            nc.vector.memset(g_pad[:, :, :], 0.0).then_inc(zeroed_dve, 1)
            dve.wait_ge(zeroed_dve, 2)
            nc.vector.memset(g_pad[:, :, E:E + 1], 1.0).then_inc(zeroed_dve, 1)
            dve.wait_ge(th_ready, 1)
            nc.vector.tensor_scalar(gates[:, 0:1], gates_th[:, 0:1], 1 / NS, None, ALU.mult).then_inc(gates_ready, 1)
            nc.vector.tensor_scalar(gates[:, 1:2], gates_th[:, 1:2], 1 / WS, None, ALU.mult).then_inc(gates_ready, 1)
            for n in range(N_MIX):
                (hi, lo), scale = mix_out(n)
                dve.wait_ge(mix_hi, n + 1)
                nc.vector.scalar_tensor_tensor(lo, mix_ps(n), scale, hi, ALU.mult, ALU.subtract
                                               ).then_inc(mix_used, 1)
            nc.vector.memset(w2_f[HLAST:128, NH - 1, :], 0.0).then_inc(zeroed_w2, 1)
            for n, (w, f) in enumerate(((w1_hl, w1_f), (w3_hl, w3_f))):
                dve.wait_ge(w_hi, n + 1)
                nc.vector.scalar_tensor_tensor(w[1][:, :, 0:HID], f, WS, w[0][:, :, 0:HID], ALU.mult, ALU.subtract
                                               ).then_inc(w_ready, 1)
            dve.wait_ge(w_hi, 3)
            nc.vector.scalar_tensor_tensor(w2_hl[1][:, :, :], w2_f, WS, w2_hl[0][:, :, :], ALU.mult, ALU.subtract
                                           ).then_inc(w_ready, 1)
            dve.wait_ge(gates_ready, 2)
            dve.wait_ge(zeroed_dve, 3)
            dve.wait_ge(consts_in, 16 * N_CONSTS)

            def carry_wait():
                nc.vector.tensor_copy(nothing[:, 1:2], nothing[:, 2:3])

            def layer_norm(n):
                for t in range(NT):
                    s = nc.vector.bn_stats(stats[0:TT, t, :], xg[0:TT, t, :])
                s.then_inc(ln_step, 1)
                dve.wait_ge(ln_step, n * 3 + 1)
                carry_wait()
                for t in range(NT):
                    s = nc.vector.bn_aggr(mv[0:TT, t, :], stats[0:TT, t, :])
                s.then_inc(ln_step, 1)
                dve.wait_ge(ln_step, n * 3 + 2)
                nc.vector.tensor_scalar(var_eps[0:TT, :], mv[0:TT, :, 1], EPS, None, ALU.add).then_inc(ln_step, 1)
                dve.wait_ge(ln_sd, n + 1)
                nc.vector.reciprocal(rstd[0:TT, :], sd[0:TT, :]).then_inc(ln_rstd, 1)
                dve.wait_ge(ln_rstd, n + 1)
                for t in range(NT):
                    nc.vector.tensor_scalar(xn[0:TT, t, :], xg[0:TT, t, :], mv[0:TT, t, 0:1], rstd[0:TT, t:t + 1],
                                            ALU.subtract, ALU.mult).then_inc(xn_ready, 1)
                for k in range(KD):
                    dve.wait_ge(xt_hi_ready, n * KD + k + 1)
                    nc.vector.tensor_tensor(xt_hl[1][:, k, :], o_ps[:, k, 0:GT], xt_hl[0][:, k, :], ALU.subtract
                                            ).then_inc(xt_ready, 1)

            def seg(b, u, n, turn):
                dve.wait_ge(a_full, turn)
                if n == 0:
                    dve.wait_ge(mask_ready, b + 1)
                carry_wait()
                j, s = n // NSEG, n % NSEG
                nc.vector.tensor_tensor_reduce(max_junk[:, :], a_ps[:, 0:SEG], mask_b[:, u, s * SEG:(s + 1) * SEG],
                                               1.0, -3e38, ALU.add, ALU.max, maxes[:, j, s:s + 1]
                                               ).then_inc(a_used, 1)
                return j, s

            def negate(b, turn):
                dve.wait_ge(a_used, turn)
                nc.vector.tensor_reduce(neg_max[:, :], maxes[:, :, :], AX.X, ALU.max, negate=True).then_inc(dve_m, 1)
                dve.wait_ge(dve_m, m_of(b) + 1)
                for at in (0, LOW):
                    s = nc.vector.tensor_scalar(neg_pad[:, at:at + NQ], neg_max[:, :], 1e28, None, ALU.min)
                s.then_inc(neg_ready, 1)

            def shift(b, u, turn):
                dve.wait_ge(a_full, turn)
                nc.vector.tensor_copy(max_hi[:, :], a_ps[0:64, 0:128]).then_inc(dve_m, 1)
                dve.wait_ge(dve_m, m_of(b) + 2)
                nc.vector.scalar_tensor_tensor(max_rest[:, :], max_hi[:, :], low_rows[:, 0:1], a_ps[0:64, 0:128],
                                               ALU.mult, ALU.add).then_inc(a_used, 1)
                dve.wait_ge(a_used, turn)
                nc.vector.tensor_tensor(shift_m[0:64, u, :].rearrange("p (j n) -> p j n", j=NQ), blocks_sb[:, :, :],
                                        max_rest[:, :].unsqueeze(1).broadcast_to([64, NQ, 128]), ALU.mult
                                        ).then_inc(shift_ready, 1)

            def normalise(b):
                dve.wait_ge(summed, b * NC + NC)
                six = o_ps[:, 0:2, 0:3 * VC].rearrange("p a (j n) -> p a j n", j=3)
                one = o_ps[:, 2, 0:VC]
                nc.vector.tensor_scalar(den[:, 0:6].rearrange("p (a j) -> p a j", a=2), six[:, :, :, DV], 1e-30, None,
                                        ALU.max)
                nc.vector.tensor_scalar(den[:, 6:7], one[:, DV:VC], 1e-30, None, ALU.max).then_inc(dve_o, 1)
                dve.wait_ge(dve_o, b * 2 + 1)
                nc.vector.reciprocal(rden[:, :], den[:, :]).then_inc(dve_o, 1)
                dve.wait_ge(dve_o, b * 2 + 2)
                for a in range(2):
                    nc.vector.tensor_tensor(o_f[:, 3 * a:3 * a + 3, :], six[:, a, :, 0:DV],
                                            rden[:, 3 * a:3 * a + 3].unsqueeze(2).broadcast_to([128, 3, DV]), ALU.mult)
                nc.vector.tensor_scalar(o_f[:, 6, :], one[:, 0:DV], rden[:, 6:7], None, ALU.mult).then_inc(o_ready, 1)

            def out_turn(b, i, j):
                lo, hi = (0, 512) if j == 0 else (512, Q)
                dve.wait_ge(ot_hi, b * N_O + j + 1)
                nc.vector.tensor_tensor(q_all[:, bass.ds(i, 1), 1, lo:hi].rearrange("p b q -> p (b q)"),
                                        a_ps[:, 0:hi - lo],
                                        q_all[:, bass.ds(i, 1), 0, lo:hi].rearrange("p b q -> p (b q)"),
                                        ALU.subtract).then_inc(a_used, 1)

            def take(kind, j, g, i, u, turn):
                b = g * GB + i
                if kind == "seg":
                    seg(b + 1, 1 - u, j, turn)
                    if j == len(SEGS) - 1:
                        negate(b + 1, turn)
                elif kind == "max":
                    shift(b + 1, 1 - u, turn)
                else:
                    out_turn(b - 1, i - 1, j)

            def batch(g, i, u, v, first, last):
                b = g * GB + i
                plan = turn_plan(not last, not first)
                turn, base = 0, turns_before(g, i)
                for k in range(NC):
                    n = b * NC + k
                    if k == 2 and not first:
                        normalise(b - 1)
                    for kind, j in plan[k][0]:
                        turn += 1
                        take(kind, j, g, i, u, base + turn)
                    dve.wait_ge(p_f_ready, n + 1)
                    nc.vector.tensor_tensor(p_hl[0:SP, k % NPB, 1, :], p_f[0:SP, k % 2, :], p_hl[0:SP, k % NPB, 0, :],
                                            ALU.subtract).then_inc(p_ready, 1)
                    for kind, j in plan[k][1]:
                        turn += 1
                        take(kind, j, g, i, u, base + turn)

            run = body_loop(dve, batch)
            with dve.Fori(0, G) as g:
                dve.wait_ge(x_in, g * 16 + 16)
                layer_norm(g * 2)
                for h in range(H):
                    dve.wait_ge(q_hi_ready, g * H + h + 1)
                    at = slice(h * T, (h + 1) * T)
                    nc.vector.scalar_tensor_tensor(q_all[:, :, 1, at],
                                                   banks[h % 4][:, 0:GT].rearrange("p (b t) -> p b t", b=GB), 1 / WS,
                                                   q_all[:, :, 0, at], ALU.mult, ALU.subtract).then_inc(q_ready, 1)
                b0 = g * GB
                turn0 = g * ((N_M + N_O) * GB)
                for n in range(len(SEGS)):
                    seg(b0, 0, n, turn0 + n + 1)
                negate(b0, turn0 + len(SEGS))
                shift(b0, 0, turn0 + N_M)
                run(g)
                normalise(b0 + GB - 1)
                for j in range(N_O):
                    out_turn(b0 + GB - 1, GB - 1, j)
                for t in range(NT):
                    if t == 0:
                        dve.wait_ge(proj_back, g * KD + KD)
                    nc.vector.scalar_tensor_tensor(xg[0:TT, t, :], banks[2 + t // 2][0:TT, (t % 2) * D:(t % 2 + 1) * D],
                                                   gates[0:TT, 0:1],
                                                   xg[0:TT, t, :], ALU.mult, ALU.add).then_inc(x2_ready, 1)
                dve.wait_ge(x2_ready, g * NT + NT)
                layer_norm(g * 2 + 1)

                r0 = g * 11

                def step(ins, n):
                    ins.then_inc(r_step, 1)
                    dve.wait_ge(r_step, r0 + n)
                flat = "p t e -> p (t e)"
                dve.wait_ge(r_exp_ready, g + 1)
                step(nc.vector.tensor_scalar(r_one[0:TT, :, :], r_exp[0:TT, :, :], 1.0, None, ALU.add), 1)
                step(nc.vector.reciprocal(score[0:TT, :, :], r_one[0:TT, :, :]), 2)
                step(nc.vector.tensor_tensor(sel[0:TT, :, :], score[0:TT, :, :],
                                             bias_sb[0:TT, :].unsqueeze(1).broadcast_to([TT, NT, E]), ALU.add), 3)
                for t in range(NT):
                    other = sel[0:TT, t, :].unsqueeze(1).broadcast_to([TT, E, E])
                    own = sel[0:TT, t, :].unsqueeze(2).broadcast_to([TT, E, E])
                    nc.vector.tensor_tensor(ahead[0:TT, t, :, :], other, own, ALU.is_gt)
                    s = nc.vector.tensor_tensor(tied[0:TT, t, :, :], other, own, ALU.is_equal)
                step(s, 4)
                step(nc.vector.tensor_tensor(tied[0:TT, :, :, :].rearrange("p t e f -> p t (e f)"),
                                             tied[0:TT, :, :, :].rearrange("p t e f -> p t (e f)"),
                                             before_sb[0:TT, :].unsqueeze(1).broadcast_to([TT, NT, E * E]),
                                             ALU.mult), 5)
                step(nc.vector.tensor_tensor(ahead[0:TT, :, :, :], ahead[0:TT, :, :, :], tied[0:TT, :, :, :],
                                             ALU.add), 6)
                step(nc.vector.tensor_reduce(rank[0:TT, :, :], ahead[0:TT, :, :, :], AX.X, ALU.add), 7)
                step(nc.vector.scalar_tensor_tensor(w_top[0:TT, :, :], rank[0:TT, :, :], TOPK - 0.5,
                                                    score[0:TT, :, :], ALU.is_lt, ALU.mult), 8)
                step(nc.vector.tensor_reduce(w_sum[0:TT, :], w_top[0:TT, :, :], AX.X, ALU.add), 9)
                step(nc.vector.tensor_scalar(w_sum[0:TT, :], w_sum[0:TT, :], 1e-12, None, ALU.max), 10)
                step(nc.vector.reciprocal(w_rec[0:TT, :], w_sum[0:TT, :]), 11)
                for at in (0, LOW):
                    s = nc.vector.tensor_tensor(g_pad[0:TT, :, at:at + E], w_top[0:TT, :, :],
                                                w_rec[0:TT, :].unsqueeze(2).broadcast_to([TT, NT, E]), ALU.mult)
                s.then_inc(gate_ready, 1)
                dve.wait_ge(g_full, g + 1)
                nc.vector.tensor_copy(g_hi[:, :], a_ps[0:64, 0:GT]).then_inc(g_ready, 1)
                dve.wait_ge(g_ready, g * 2 + 1)
                nc.vector.scalar_tensor_tensor(g_t[0:64, :], g_hi[:, :], low_rows[:, 0:1], a_ps[0:64, 0:GT],
                                               ALU.mult, ALU.add).then_inc(g_ready, 1)
                for j in range(NH):
                    n = g * NH + j
                    dve.wait_ge(silu_ready, n + 1)
                    if j >= 2:
                        dve.wait_ge(h_used, n - 1)
                    nc.vector.tensor_tensor(v_f[:, 0, :], sc_ps[j % 2][:, 1, 0:GT], s_f[:, j % 2, :], ALU.mult
                                            ).then_inc(h_step, 1)
                    dve.wait_ge(h_step, n * 3 + 1)
                    nc.vector.scalar_tensor_tensor(v_f[:, 1, :], v_f[:, 0, :], 1 / WS, o_ps[:, j % 2, 0:GT],
                                                   ALU.mult, ALU.mult).then_inc(h_step, 1)
                    dve.wait_ge(h_step, n * 3 + 2)
                    nc.vector.tensor_copy(h_hl[:, j % 2, 0, 0:GT], v_f[:, 1, :]).then_inc(h_step, 1)
                    dve.wait_ge(h_step, n * 3 + 3)
                    nc.vector.tensor_tensor(h_hl[:, j % 2, 1, 0:GT], v_f[:, 1, :], h_hl[:, j % 2, 0, 0:GT],
                                            ALU.subtract).then_inc(h_ready, 1)
                dve.wait_ge(h_used, g * NH + NH)
                for t in range(NT):
                    acc = (o_ps[0:TT, 2, :] if t < 2 else a_ps[0:TT, :])[:, (t % 2) * D:(t % 2 + 1) * D]
                    nc.vector.scalar_tensor_tensor(xg[0:TT, t, :], acc, gates[0:TT, 1:2], xg[0:TT, t, :],
                                                   ALU.mult, ALU.add).then_inc(y_ready, 1)

        @block.tensor
        def _(pe):
            def product(outs, lhs, rhs, first=True, last=True, **kw):
                mm = None
                for n, (a, c) in enumerate(((0, 0), (0, 1), (1, 0))):
                    mm = nc.tensor.matmul(outs, lhs[a], rhs[c], start=first and n == 0, stop=last and n == 2, **kw)
                return mm

            pe.sem_inc(scored, 1)
            pe.wait_ge(wq_in, 32)
            for n in range(N_MIX):
                h = n % H
                if n == H:
                    pe.wait_ge(wo_in, 32)
                if n >= 4:
                    pe.wait_ge(mix_used, n - 3)
                if n < H:
                    for k in range(KD):
                        mm = nc.tensor.matmul(mix_ps(n)[:, k, :], wq_f[:, h, k * 128:(k + 1) * 128],
                                              wk_f[:, h // 2, :], start=True, stop=True)
                else:
                    mm = nc.tensor.matmul(mix_ps(n), wv_f[:, h // 2, :], wo_f[:, h, :], start=True, stop=True)
                mm.then_inc(mix_made, 1)
            pe.wait_ge(w_ready, 3)
            pe.wait_ge(zeroed, N_ZERO)
            pe.wait_ge(consts_in, 16 * N_CONSTS)

            def layer_norm(n):
                pe.wait_ge(xn_ready, n * NT + NT)
                for k in range(KD):
                    for t in range(NT):
                        mm = nc.tensor.transpose(o_ps[:, k, t * TT:(t + 1) * TT], xn[0:TT, t, k * 128:(k + 1) * 128],
                                                 id_sb[0:TT, 0:TT])
                    mm.then_inc(xt_full, 1)
                pe.wait_ge(xt_ready, n * KD + KD)

            def take(kind, j, g, i, u, v, turn, turn_free=True):
                b = g * GB + i
                if turn_free:
                    pe.wait_ge(a_used, turn - 1)
                if kind == "seg":
                    if j == 0:
                        pe.wait_ge(ct_hi_ready, b + 2)
                        pe.wait_ge(staged[1 - u], (v + u + 1) * 16)
                    t, s = j // NSEG, j % NSEG
                    mm = nc.tensor.matmul(a_ps[:, 0:SEG], q_st[:, 1 - u, 0, t * 128:(t + 1) * 128],
                                          ct[1 - u][0][:, s * SEG:(s + 1) * SEG], start=True, stop=True)
                elif kind == "max":
                    pe.wait_ge(neg_ready, b + 2)
                    mm = nc.tensor.transpose(a_ps[:, 0:128], neg_pad[:, :], id_sb[:, :])
                else:
                    if j == 0:
                        pe.wait_ge(o_ready, b)
                    for t in (range(0, 4) if j == 0 else range(4, NQ)):
                        mm = nc.tensor.transpose(a_ps[:, (t % 4) * 128:(t % 4 + 1) * 128], o_f[:, t, :], id_sb[:, :])
                mm.then_inc(a_full, 1)

            def scores(b, k, u, v, first):
                n = b * NC + k
                if not (first and k < 2):
                    pe.wait_ge(p_f_ready, n - 1)
                if k == 0:
                    pe.wait_ge(shift_ready, b + 2)
                    pe.wait_ge(row_in[u], v * 16 + 32)
                    pe.wait_ge(split_done, b * 2 + 1)
                keys_k = slice(k * SP, (k + 1) * SP)
                for a in range(2):
                    nc.tensor.matmul(sc_ps[k % 2][0:SP, a, 0:HALF], shift_w[:, u, keys_k],
                                     shift_m[:, u, a * HALF:(a + 1) * HALF], start=True, stop=False)
                for n_pass, (kp, qp) in enumerate(((0, 0), (0, 1), (1, 0))):
                    for a in range(2):
                        mm = nc.tensor.matmul(sc_ps[k % 2][0:SP, a, 0:HALF], ct[u][kp][:, keys_k],
                                              q_st[:, u, qp, a * HALF:(a + 1) * HALF], start=False, stop=n_pass == 2)
                mm.then_inc(scored, 1)

            def weighted(b, k, u, first):
                pe.wait_ge(p_ready, b * NC + k + 1)
                if k == 0:
                    pe.wait_ge(split_done, b * 2 + 2)
                    if not first:
                        pe.wait_ge(o_ready, b)
                hi, lo = p_hl[0:SP, k % NPB, 0, :], p_hl[0:SP, k % NPB, 1, :]
                for t in range(NQ):
                    q = slice(t * 128, (t + 1) * 128)
                    to = o_ps[:, t // 3, (t % 3) * VC:(t % 3 + 1) * VC]
                    for n, (p, c, w) in enumerate(((hi, 0, VC), (hi, VC, DV), (lo, 0, VC))):
                        mm = nc.tensor.matmul(to[:, 0:w], p[:, q], cv[u][0:SP, k, c:c + w],
                                              start=k == 0 and t % 3 == 0 and n == 0, stop=k == NC - 1 and n == 2,
                                              skip_group_check=True)
                mm.then_inc(summed, 1)

            def batch(g, i, u, v, first, last):
                b = g * GB + i
                plan = turn_plan(not last, not first)
                turn, base = 0, turns_before(g, i)
                for k in range(NC):
                    scores(b, k, u, v, first)
                    for kind, j in plan[k][0]:
                        turn += 1
                        take(kind, j, g, i, u, v, base + turn)
                    if k >= 2:
                        weighted(b, k - 2, u, first)
                    elif not first:
                        weighted(b - 1, NC - 2 + k, 1 - u, False)
                    for kind, j in plan[k][1]:
                        turn += 1
                        take(kind, j, g, i, u, v, base + turn)

            run = body_loop(pe, batch)
            with pe.Fori(0, G) as g:
                layer_norm(g * 2)
                for h in range(H):
                    if h >= 4:
                        pe.wait_ge(q_ready, g * H + h - 3)
                    for k in range(KD):
                        mm = product(banks[h % 4][:, 0:GT], [m[:, k, h, :] for m in m_hl],
                                     [xt[:, k, :] for xt in xt_hl], k == 0, k == KD - 1)
                    mm.then_inc(q_full, 1)
                b0 = g * GB
                turn0 = g * ((N_M + N_O) * GB)
                pe.wait_ge(q_ready, g * H + H)
                for n, (kind, j) in enumerate(SEGS + [("max", 0)]):
                    take(kind, j, g, -1, 1, g * (GB // 2) - 1, turn0 + n + 1, n > 0)
                run(g)
                for k in (NC - 2, NC - 1):
                    weighted(b0 + GB - 1, k, 1, False)
                for j in range(N_O):
                    take("out", j, g, GB, 0, 0, turn0 + (N_M + N_O) * GB - N_O + j + 1)
                pe.wait_ge(a_used, turn0 + (N_M + N_O) * GB)
                for k in range(KD):
                    for h in range(H):
                        ot = [q_all[:, :, p, h * T:(h + 1) * T] for p in range(2)]
                        mm = product(banks[k][:, 0:GT], [n_[:, h, k * 128:(k + 1) * 128] for n_ in n_hl], ot,
                                     h == 0, h == H - 1)
                    mm.then_inc(proj_full, 1)
                for k in range(KD):
                    pe.wait_ge(proj_copied, g * KD + k + 1)
                    for t in range(NT):
                        mm = nc.tensor.transpose(banks[2 + t // 2][0:TT, (t % 2) * D + k * 128:(t % 2) * D + (k + 1) * 128],
                                                 proj_t[:, k, t * TT:(t + 1) * TT], id_sb[:, :])
                    mm.then_inc(proj_back, 1)
                layer_norm(g * 2 + 1)
                for t in range(NT):
                    for k in range(KD):
                        mm = nc.tensor.matmul(a_ps[0:TT, t * E:(t + 1) * E], xt_f[:, k, t * TT:(t + 1) * TT],
                                              gate_sb[:, k, :], start=k == 0, stop=k == KD - 1)
                mm.then_inc(logits_full, 1)
                pe.wait_ge(gate_ready, g + 1)
                for t in range(NT):
                    mm = nc.tensor.transpose(a_ps[:, t * TT:(t + 1) * TT], g_pad[0:TT, t, :], id_sb[0:TT, 0:TT])
                mm.then_inc(g_full, 1)
                pe.wait_ge(g_ready, g * 2 + 2)

                def down(j):
                    pe.wait_ge(h_ready, g * NH + j + 1)
                    for t in range(NT):
                        acc = (o_ps[0:TT, 2, :] if t < 2 else a_ps[0:TT, :])[:, (t % 2) * D:(t % 2 + 1) * D]
                        hid = [h_hl[:, j % 2, p, t * TT:(t + 1) * TT] for p in range(2)]
                        mm = product(acc, hid, [w[:, j, :] for w in w2_hl], j == 0 and t % 2 == 0, j == NH - 1,
                                     skip_group_check=True)
                    mm.then_inc(h_used, 1)

                for j in range(NH):
                    if j >= 2:
                        pe.wait_ge(h_ready, g * NH + j - 1)
                    hid = slice(j * 128, (j + 1) * 128)
                    for a, w in enumerate((w1_hl, w3_hl)):
                        for k in range(KD):
                            product(sc_ps[j % 2][:, a, 0:GT], [p[:, k, hid] for p in w], [xt[:, k, :] for xt in xt_hl],
                                    k == 0, k == KD - 1)
                    nc.tensor.matmul(o_ps[:, j % 2, 0:GT], expand_sb[:, hid], g_t[:, :], start=True, stop=True
                                     ).then_inc(h_full, 1)
                    if j >= 1:
                        down(j - 1)
                down(NH - 1)
                pe.wait_ge(y_ready, g * NT + NT)


def kernel(x, ctx_1024, mask_BxS2_bf1, g_xattn, g_ffn, L0_xattn_Wq, L0_xattn_Wk, L0_xattn_Wv, L0_xattn_Wo,
           L0_ffn_gate_w, L0_ffn_router_bias, L0_ffn_W1, L0_ffn_W3, L0_ffn_W2, L0_ffn_sw1, L0_ffn_sw3, L0_ffn_sw2):
    import numpy as np
    import concourse.bacc as bacc
    from concourse import mybir as mb
    from concourse.bass_utils import run_bass_kernel_spmd as launch

    def lay(a):
        return np.ascontiguousarray(a)

    ctx_h = np.asarray(ctx_1024)
    mask_h = np.asarray(mask_BxS2_bf1).view(np.uint8)
    blocks = np.zeros((64, NQ, 128), mb.dt.np(BF16))
    for j in range(NQ):
        blocks[j, j], blocks[LOW + j, j] = 1, 1
    expand = np.zeros((128, NH * 128), np.float16)
    for j in range(HID):
        e = min(j // INTER, E)
        expand[e, j] = 1
        if e < E:
            expand[LOW + e, j] = 1
    before = np.zeros((128, E * E), np.float32)
    for e in range(E):
        before[:, e * E:e * E + e] = 1
    low = np.zeros((64, 1), np.float32)
    low[LOW:] = -1
    w1, w3, w2 = np.asarray(L0_ffn_W1), np.asarray(L0_ffn_W3), np.asarray(L0_ffn_W2)
    arrays = {
        "x": lay(np.asarray(x).reshape(B * T, D)),
        "ctx": lay(ctx_h),
        "ctxT": lay(ctx_h.reshape(B, SP, NC, DV).transpose(0, 3, 2, 1).reshape(B, DV, S)),
        "mask": lay(mask_h.reshape(B, SP, NC).transpose(0, 2, 1).reshape(B, S)),
        "g_xattn": lay(g_xattn), "g_ffn": lay(g_ffn),
        "wqT": lay(np.asarray(L0_xattn_Wq).T.reshape(H, DH, D)),
        "wkT": lay(np.asarray(L0_xattn_Wk).T.reshape(KV, DH, DV)),
        "wvT": lay(np.asarray(L0_xattn_Wv).T.reshape(KV, DH, DV)),
        "wo": lay(np.asarray(L0_xattn_Wo).reshape(H, DH, D)),
        "gateT": lay(np.asarray(L0_ffn_gate_w).T),
        "rbias": lay(L0_ffn_router_bias),
        "w1": lay(np.concatenate([w1.transpose(1, 0, 2).reshape(D, E * INTER), np.asarray(L0_ffn_sw1).T], 1)),
        "w3": lay(np.concatenate([w3.transpose(1, 0, 2).reshape(D, E * INTER), np.asarray(L0_ffn_sw3).T], 1)),
        "w2": lay(np.concatenate([w2.reshape(E * INTER, D), np.asarray(L0_ffn_sw2).T], 0)),
        "ident": np.eye(128, dtype=np.float32), "blocks": blocks, "expand": expand, "before": before, "low": low,
    }
    nc = bacc.Bacc("TRN2", target_bir_lowering=False, num_devices=1)
    aps = {n: nc.dram_tensor(f"in_{n}", a.shape, mb.dt.from_np(a.dtype), kind="ExternalInput").ap()
           for n, a in arrays.items()}
    out = nc.dram_tensor("out", (B * T, D), F32, kind="ExternalOutput").ap()
    build(nc, **aps, out=out)
    r = launch(nc, [{f"in_{n}": a for n, a in arrays.items()}], core_ids=[0])
    return r.results[0]["out"].reshape(B, T, D)
```

```python
from contextlib import ExitStack

import concourse.bass as bass
from concourse import mybir

F32, F16, BF16, U8 = mybir.dt.float32, mybir.dt.float16, mybir.dt.bfloat16, mybir.dt.uint8
ACT = mybir.ActivationFunctionType
ALU = mybir.AluOpType
AX = mybir.AxisListType

B, T, D = 32, 56, 256
S, DV = 1500, 128
H, KV, DH = 16, 8, 128
E, TOPK, INTER, NSH = 8, 2, 176, 352
NC = 12
SP = S // NC
Q = H * T
NQ = Q // 128
HALF = Q // 2
NSEG, SEG = 3, S // 3
GB = 8
G = B // GB
GT = GB * T
NT, TT = 4, GT // 4
KD = D // 128
HID = E * INTER + NSH
NH = -(-HID // 128)
HLAST = HID - (NH - 1) * 128
VC = DV + 1
CUT = 512 - 3 * VC
EPS = 1e-5
MASKED = -1e30
WS = 64.0
NS = 256.0
LOW = 32
NPB = 4
LAG = 3

SEG_SLOTS = [(), (2, 3), (0, 2), (0, 2), (0, 2), (0, 2), (0, 2, 3), (0, 2), (0, 2), (0, 2, 3), (0,), ()]
OUT_SLOTS, MAX_SLOT, ROW_SLOTS = ((4, 1), (5, 1)), (11, 0), ((11, 2), (11, 3))
KEY_STEPS = {(0, 0): ("ct", 0), (0, 2): ("mask", 0), (1, 2): ("ct", 1), (2, 2): ("mask", 1), (3, 2): ("ct", 2),
             (4, 2): ("mask", 2), (6, 2): ("c", 0)}
POOL_CT, POOL_C = 4, 7
N_SEG = NQ * NSEG
N_M, N_O = N_SEG + 1 + len(ROW_SLOTS), len(OUT_SLOTS)


PROLOGUE = [("seg", j) for j in range(N_SEG)] + [("max", 0), ("row", 0), ("row", 1)]


def turn_plan(has_next, has_last):
    plan, n = [[[] for _ in range(4)] for _ in range(NC)], 0
    for k in range(NC):
        for slot in SEG_SLOTS[k] if has_next else ():
            plan[k][slot].append(("seg", n))
            n += 1
    assert n == (N_SEG if has_next else 0)
    if has_next:
        plan[MAX_SLOT[0]][MAX_SLOT[1]].append(("max", 0))
        for j, (k, slot) in enumerate(ROW_SLOTS):
            plan[k][slot].append(("row", j))
    if has_last:
        for j, (k, slot) in enumerate(OUT_SLOTS):
            plan[k][slot].append(("out", j))
    return plan


def build(nc, x, ctx, ctxT, mask, maskT, g_xattn, g_ffn, wqT, wkT, wvT, wo, gateT, rbias, w1, w3, w2, ident, pick,
          expand, before, low, out):
    with ExitStack() as stack:
        def sb(name, shape, dt):
            return stack.enter_context(nc.sbuf_tensor(name, shape, dt))

        def ps(name, shape, dt):
            return stack.enter_context(nc.psum_tensor(name, shape, dt))

        def sem(name):
            return stack.enter_context(nc.semaphore(name))

        sc_ps = [ps(f"sc_ps{i}", [128, 2, 512], F32) for i in range(2)]
        o_ps = ps("o_ps", [128, 2, 512], F32)
        a_ps = ps("a_ps", [128, 2, 512], F32)

        m_hl = [sb(f"m_{p}", [128, KD, H, 128], F16) for p in ("hi", "lo")]
        n_hl = [sb(f"n_{p}", [128, H, D], F16) for p in ("hi", "lo")]
        w1_hl = [sb(f"w1_{p}", [128, KD, NH * 128], F16) for p in ("hi", "lo")]
        w3_hl = [sb(f"w3_{p}", [128, KD, NH * 128], F16) for p in ("hi", "lo")]
        w2_hl = [sb(f"w2_{p}", [128, NH, D], F16) for p in ("hi", "lo")]
        gate_sb = sb("gate_sb", [128, KD, E], F32)
        bias_sb = sb("bias_sb", [128, E], F32)
        id_sb = sb("id_sb", [128, 128], F32)
        pick_sb = sb("pick_sb", [128, NQ, 128], BF16)
        expand_sb = sb("expand_sb", [128, NH * 128], F16)
        before_sb = sb("before_sb", [128, E * E], F32)
        gates_in = sb("gates_in", [128, 2], F32)
        gates_th = sb("gates_th", [128, 2], F32)
        gates = sb("gates", [128, 2], F32)
        nothing = sb("nothing", [128, 5], F32)
        low_rows = sb("low_rows", [64, 1], F32)

        q_all = sb("q_all", [128, GB, 2, Q], F16)
        q_st = sb("q_st", [128, 2, 2, Q], F16)

        c_f = sb("c_f", [128, NC, DV], F32)
        ct_f = sb("ct_f", [128, S], F32)
        mask_u8 = sb("mask_u8", [128, S], U8)
        keys = sb("keys", [128, 2, 2 * S + NC * (VC + DV)], F16)
        ct = [[keys[:, u, p * S:(p + 1) * S] for p in range(2)] for u in range(2)]
        cv = [keys[:, u, 2 * S:].rearrange("p (c n) -> p c n", c=NC) for u in range(2)]
        mask_n = sb("mask_n", [128, NC], U8)
        mask_b = sb("mask_b", [128, S], BF16)
        mask_c = sb("mask_c", [128, 2, NC], F32)
        shift_m = sb("shift_m", [128, 128], BF16)
        shift_b = sb("shift_b", [128, 2, Q], F32)

        p_f = sb("p_f", [128, 2, Q], F32)
        p_hl = sb("p_hl", [128, NPB, 2, Q], F16)
        h_hl = p_hl
        s_f = p_f[:, 0, :].rearrange("p (u n) -> p u n", u=2)
        v_f = p_f[:, 1, :].rearrange("p (u n) -> p u n", u=2)
        maxes = sb("maxes", [128, NQ, NSEG], F32)
        neg_max = sb("neg_max", [128, NQ], F32)
        neg_pad = sb("neg_pad", [128, 128], F32)
        max_hi = sb("max_hi", [64, 128], BF16)
        den = sb("den", [128, NQ], F32)
        rden = sb("rden", [128, NQ], F32)
        o_f = sb("o_f", [128, NQ, DV], F32)

        xg = sb("xg", [128, NT, D], F32)
        xn = sb("xn", [128, NT, D], F32)
        max_junk = [xn[:, 2 * a:2 * a + 2, :].rearrange("p t d -> p (t d)")[:, 0:SEG] for a in range(2)]
        xt_f = o_f[:, :, :].rearrange("p j d -> p (j d)").rearrange("p (k n) -> p k n", k=KD)
        xt_hl = [sb(f"xt_{p}", [128, KD, GT], F16) for p in ("hi", "lo")]
        proj_t = xt_f
        stats = sb("stats", [128, NT, 6], F32)
        mv = sb("mv", [128, NT, 2], F32)
        var_eps = sb("var_eps", [128, NT], F32)
        sd = sb("sd", [128, NT], F32)
        rstd = sb("rstd", [128, NT], F32)
        r_exp = sb("r_exp", [128, NT, E], F32)
        r_one = sb("r_one", [128, NT, E], F32)
        score = sb("score", [128, NT, E], F32)
        sel = sb("sel", [128, NT, E], F32)
        ahead, tied = [xn[:, a, :].rearrange("p (t e f) -> p t e f", t=NT, e=E) for a in range(2)]
        rank = sb("rank", [128, NT, E], F32)
        w_top = sb("w_top", [128, NT, E], F32)
        w_sum = sb("w_sum", [128, NT], F32)
        w_rec = sb("w_rec", [128, NT], F32)
        g_pad = sb("g_pad", [128, NT, 128], F32)
        g_hi = sb("g_hi", [64, GT], F16)
        g_t = sb("g_t", [128, GT], F16)

        consts_in = sem("consts_in")
        wq_in = sem("wq_in")
        wo_in = sem("wo_in")
        w13_in = sem("w13_in")
        w2_in = sem("w2_in")
        zeroed = sem("zeroed")
        zeroed_dve = sem("zeroed_dve")
        zeroed_w2 = sem("zeroed_w2")
        mix_made = sem("mix_made")
        mix_hi = sem("mix_hi")
        mix_used = sem("mix_used")
        w_hi = sem("w_hi")
        w_ready = sem("w_ready")
        th_ready = sem("th_ready")
        gates_ready = sem("gates_ready")

        ctx_in = sem("ctx_in")
        staged = [sem(f"staged{u}") for u in range(2)]
        mask_ready = sem("mask_ready")
        ct_hi_ready = sem("ct_hi_ready")
        c_hi_ready = sem("c_hi_ready")
        split_done = sem("split_done")
        scored = sem("scored")
        shifted = sem("shifted")
        p_hi_ready = sem("p_hi_ready")
        p_f_ready = sem("p_f_ready")
        p_ready = sem("p_ready")
        summed = sem("summed")
        a_full = sem("a_full")
        a_used = sem("a_used")
        neg_ready = sem("neg_ready")
        o_ready = sem("o_ready")
        ot_hi = sem("ot_hi")
        dve_m = sem("dve_m")
        dve_o = sem("dve_o")

        x_in = sem("x_in")
        ln_step = sem("ln_step")
        ln_sd = sem("ln_sd")
        ln_rstd = sem("ln_rstd")
        xn_ready = sem("xn_ready")
        xt_full = sem("xt_full")
        xt_hi_ready = sem("xt_hi_ready")
        xt_ready = sem("xt_ready")
        q_full = sem("q_full")
        q_hi_ready = sem("q_hi_ready")
        q_ready = sem("q_ready")
        proj_full = sem("proj_full")
        proj_copied = sem("proj_copied")
        proj_back = sem("proj_back")
        x2_ready = sem("x2_ready")
        logits_full = sem("logits_full")
        r_exp_ready = sem("r_exp_ready")
        r_step = sem("r_step")
        gate_ready = sem("gate_ready")
        g_full = sem("g_full")
        g_ready = sem("g_ready")
        h_full = sem("h_full")
        silu_ready = sem("silu_ready")
        h_step = sem("h_step")
        h_ready = sem("h_ready")
        h_used = sem("h_used")
        y_ready = sem("y_ready")
        stored = sem("stored")

        room1 = q_all[:].rearrange("p b u q -> p (b u q)").bitcast(F32)
        room2 = keys[:].rearrange("p u n -> p (u n)").bitcast(F32)
        wq_f = room1[:, 0:H * D].rearrange("p (h n) -> p h n", h=H)
        wk_f = room1[:, H * D:H * D + KV * DV].rearrange("p (h n) -> p h n", h=KV)
        wo_f = room2[:, 0:H * D].rearrange("p (h n) -> p h n", h=H)
        wv_f = room2[:, H * D:H * D + KV * DV].rearrange("p (h n) -> p h n", h=KV)
        w1_f = room1[:, 0:KD * HID].rearrange("p (k n) -> p k n", k=KD)
        w3_f = room1[:, KD * HID:2 * KD * HID].rearrange("p (k n) -> p k n", k=KD)
        w2_f = room2[:, 0:NH * D].rearrange("p (t n) -> p t n", t=NH)
        banks = [sc_ps[0][:, 0, :], sc_ps[0][:, 1, :], sc_ps[1][:, 0, :], sc_ps[1][:, 1, :]]

        N_CONSTS = 9
        N_ZERO = 6
        N_MIX = 2 * H

        def mix_out(n):
            h = n % H
            return [(m_hl[p][:, :, h, :] if n < H else n_hl[p][:, h, :]) for p in range(2)], \
                (WS / DH ** 0.5 if n < H else NS)

        def mix_ps(n):
            b = banks[n % 4][:, 0:2 * 128]
            return b.rearrange("p (k n) -> p k n", k=KD) if n < H else b

        def turns_before(g, i):
            return g * ((N_M + N_O) * GB) + (i * (N_M + N_O) + (N_M if isinstance(i, int) and i == 0 else N_M - N_O))

        STEPS_M = 2

        def m_of(b):
            return b * STEPS_M

        def body_loop(eng, per_batch):
            def run(g):
                half = g * (GB // 2)
                per_batch(g, 0, 0, half, True, False)
                with eng.Fori(0, (GB - 2) // 2) as r:
                    per_batch(g, r * 2 + 1, 1, half + r, False, False)
                    per_batch(g, r * 2 + 2, 0, half + r + 1, False, False)
                per_batch(g, GB - 1, 1, half + (GB // 2 - 1), False, True)
            return run

        block = stack.enter_context(nc.Block())


        @block.sync
        def _(sp):
            sp.dma_start(wq_f, wqT.rearrange("h e n -> e h n")).then_inc(wq_in, 16)
            sp.dma_start(wk_f, wkT.rearrange("h e n -> e h n")).then_inc(wq_in, 16)
            sp.dma_start(wo_f, wo.rearrange("h e n -> e h n")).then_inc(wo_in, 16)
            sp.dma_start(wv_f, wvT.rearrange("h e n -> e h n")).then_inc(wo_in, 16)
            sp.dma_start(id_sb[:, :], ident).then_inc(consts_in, 16)
            sp.dma_start(pick_sb[:, :, :], pick).then_inc(consts_in, 16)
            sp.dma_start(expand_sb[:, :], expand).then_inc(consts_in, 16)
            sp.dma_start(before_sb[:, :], before).then_inc(consts_in, 16)
            sp.dma_start(gate_sb[:, :, :], gateT.rearrange("(k p) e -> p k e", k=KD)).then_inc(consts_in, 16)
            sp.dma_start(bias_sb[:, :], rbias.partition_broadcast(128)).then_inc(consts_in, 16)
            sp.dma_start(gates_in[:, 0:1], g_xattn.partition_broadcast(128)).then_inc(consts_in, 16)
            sp.dma_start(gates_in[:, 1:2], g_ffn.partition_broadcast(128)).then_inc(consts_in, 16)
            sp.dma_start(low_rows[:, :], low).then_inc(consts_in, 16)
            sp.wait_ge(mix_used, H)
            sp.dma_start(w1_f, w1.rearrange("(k p) n -> p k n", k=KD)).then_inc(w13_in, 16)
            sp.dma_start(w3_f, w3.rearrange("(k p) n -> p k n", k=KD)).then_inc(w13_in, 16)
            sp.wait_ge(mix_used, 2 * H)
            sp.dma_start(w2_f[:, 0:NH - 1, :], w2[0:(NH - 1) * 128, :].rearrange("(t p) n -> p t n", p=128)
                         ).then_inc(w2_in, 16)
            sp.dma_start(w2_f[0:HLAST, NH - 1, :], w2[(NH - 1) * 128:HID, :]).then_inc(w2_in, 16)

            def batch(g, i, u, v, first, last):
                b = g * GB + i
                sp.wait_ge(split_done, b * 2 + 1)
                sp.dma_start(ct_f[:, :], ctxT[bass.ds(b, 1)].rearrange("b d s -> (b d) s")).then_inc(ctx_in, 16)
                sp.dma_start(mask_u8[:, :], maskT[bass.ds(b, 1), :].rearrange("b s -> (b s)").partition_broadcast(128)
                             ).then_inc(ctx_in, 16)
                sp.dma_start(mask_n[0:SP, :], mask[bass.ds(b, 1), :].rearrange("b (p c) -> (b p) c", c=NC)
                             ).then_inc(ctx_in, 16)
                sp.dma_start(c_f[0:SP, :, :], ctx[bass.ds(b, 1)].rearrange("b (p c) d -> (b p) c d", c=NC)
                             ).then_inc(ctx_in, 16)
                sp.wait_ge(q_ready, g * H + H)
                if not first:
                    sp.wait_ge(scored, b * NC - NC + 1)
                sp.dma_start(q_st[:, u, :, :], q_all[:, bass.ds(i, 1), :, :].rearrange("p b u q -> p (b u) q")
                             ).then_inc(staged[u], 16)

            run = body_loop(sp, batch)
            with sp.Fori(0, G) as g:
                run(g)

        @block.gpsimd
        def _(pool):
            pool.sem_inc(split_done, 1)
            nc.gpsimd.memset(w1_hl[0][:, :, HID:], 0.0).then_inc(zeroed, 1)
            nc.gpsimd.memset(w1_hl[1][:, :, HID:], 0.0).then_inc(zeroed, 1)
            nc.gpsimd.memset(w3_hl[0][:, :, HID:], 0.0).then_inc(zeroed, 1)
            nc.gpsimd.memset(w3_hl[1][:, :, HID:], 0.0).then_inc(zeroed, 1)
            nc.gpsimd.memset(g_t[:, :], 0.0).then_inc(zeroed, 1)
            pool.wait_ge(zeroed, 5)
            pool.wait_ge(w_ready, 3)
            for u in range(2):
                last = nc.gpsimd.memset(cv[u][:, :, DV:VC], 1.0)
            last.then_inc(zeroed, 1)
            pool.wait_ge(zeroed, N_ZERO)

            def split_ct(b, u):
                pool.wait_ge(ct_hi_ready, b * NSEG + NSEG)
                nc.gpsimd.tensor_tensor(ct[u][1], ct_f[:, :], ct[u][0], ALU.subtract).then_inc(split_done, 1)

            def split_c(b, u):
                pool.wait_ge(c_hi_ready, b + 1)
                nc.gpsimd.tensor_tensor(cv[u][0:SP, :, VC:], c_f[0:SP, :, :], cv[u][0:SP, :, 0:DV], ALU.subtract
                                        ).then_inc(split_done, 1)

            def batch(g, i, u, v, first, last):
                b = g * GB + i
                for k in range(NC):
                    pool.wait_ge(p_f_ready, b * NC + k + 1)
                    nc.gpsimd.tensor_tensor(p_hl[0:SP, k % NPB, 1, :], p_f[0:SP, k % 2, :], p_hl[0:SP, k % NPB, 0, :],
                                            ALU.subtract).then_inc(p_ready, 1)
                    if not last and k == POOL_CT:
                        split_ct(b + 1, 1 - u)
                    if not last and k == POOL_C:
                        split_c(b + 1, 1 - u)

            run = body_loop(pool, batch)
            with pool.Fori(0, G) as g:
                split_ct(g * GB, 0)
                split_c(g * GB, 0)
                run(g)

        @block.scalar
        def _(act):
            act.sem_inc(stored, 16)
            act.wait_ge(consts_in, 16 * N_CONSTS)
            nc.scalar.activation(gates_th[:, :], gates_in[:, :], ACT.Tanh).then_inc(th_ready, 1)
            for n in range(N_MIX):
                (hi, _), scale = mix_out(n)
                act.wait_ge(mix_made, n + 1)
                nc.scalar.activation(hi, mix_ps(n), ACT.Copy, scale=scale).then_inc(mix_hi, 1)
            act.wait_ge(w13_in, 32)
            nc.scalar.activation(w1_hl[0][:, :, 0:HID], w1_f, ACT.Copy, scale=WS).then_inc(w_hi, 1)
            nc.scalar.activation(w3_hl[0][:, :, 0:HID], w3_f, ACT.Copy, scale=WS).then_inc(w_hi, 1)
            act.wait_ge(w2_in, 32)
            act.wait_ge(zeroed_w2, 1)
            nc.scalar.activation(w2_hl[0][:, :, :], w2_f, ACT.Copy, scale=WS).then_inc(w_hi, 1)

            def layer_norm(n):
                act.wait_ge(ln_step, n * 3 + 3)
                nc.scalar.activation(sd[0:TT, :], var_eps[0:TT, :], ACT.Sqrt).then_inc(ln_sd, 1)
                for k in range(KD):
                    act.wait_ge(xt_full, n * KD + k + 1)
                    nc.scalar.activation(xt_f[:, k, :], o_ps[:, k, 0:GT], ACT.Copy)
                    nc.scalar.activation(xt_hl[0][:, k, :], o_ps[:, k, 0:GT], ACT.Copy).then_inc(xt_hi_ready, 1)

            def split_ct(b, u, first, s):
                if s == 0:
                    act.wait_ge(ctx_in, b * 64 + 64)
                    if not first:
                        act.wait_ge(scored, b * NC - NC + 1)
                at = slice(s * SEG, (s + 1) * SEG)
                nc.scalar.activation(ct[u][0][:, at], ct_f[:, at], ACT.Copy).then_inc(ct_hi_ready, 1)

            def split_c(b, u, first):
                if not first:
                    act.wait_ge(summed, b * NC - NC)
                nc.scalar.activation(cv[u][0:SP, :, 0:DV], c_f[0:SP, :, :], ACT.Copy).then_inc(c_hi_ready, 1)

            def masks(b, u, s):
                if s == 0:
                    act.wait_ge(neg_ready, b + 1)
                if s == NSEG - 1:
                    nc.scalar.activation(mask_c[0:SP, u, :], mask_n[0:SP, :], ACT.Copy, scale=-MASKED, bias=MASKED)
                at = slice(s * SEG, (s + 1) * SEG)
                nc.scalar.activation(mask_b[:, at], mask_u8[:, at], ACT.Copy, scale=-MASKED, bias=MASKED
                                     ).then_inc(mask_ready, 1)

            def out_turn(b, j, turn, a):
                lo, hi = (0, 512) if j == 0 else (512, Q)
                act.wait_ge(a_full, turn)
                nc.scalar.activation(q_all[:, bass.ds(b[1], 1), 0, lo:hi].rearrange("p b q -> p (b q)"),
                                     a_ps[:, a, 0:hi - lo], ACT.Copy).then_inc(ot_hi, 1)

            def batch(g, i, u, v, first, last):
                b = g * GB + i
                plan = turn_plan(not last, not first)
                turn, base = [0], turns_before(g, i)

                def fill(k, slots):
                    for kind, j in sum([plan[k][slot] for slot in slots], []):
                        turn[0] += 1
                        if kind == "out":
                            out_turn((b, i - 1), j, base + turn[0], (turn[0] - 1) % 2)

                def next_keys(k, step):
                    kind, s = KEY_STEPS.get((k, step), ("", 0)) if not last else ("", 0)
                    if kind == "ct":
                        split_ct(b + 1, 1 - u, first, s)
                    elif kind == "mask":
                        masks(b + 1, 1 - u, s)
                    elif kind == "c":
                        split_c(b + 1, 1 - u, first)

                for k in range(NC):
                    n = b * NC + k
                    fill(k, (0, 1))
                    next_keys(k, 0)
                    act.wait_ge(shifted, n + 1)
                    if not (first and k < NPB):
                        act.wait_ge(summed, n - NPB + 1)
                    scores = sc_ps[k % 2][0:SP, :, 0:HALF]
                    nc.scalar.activation(p_hl[0:SP, k % NPB, 0, :].rearrange("p (a n) -> p a n", a=2), scores,
                                         ACT.Exp).then_inc(p_hi_ready, 1)
                    next_keys(k, 1)
                    if not (first and k < 2):
                        act.wait_ge(p_ready, n - 1)
                    nc.scalar.activation(p_f[0:SP, k % 2, :].rearrange("p (a n) -> p a n", a=2), scores,
                                         ACT.Exp).then_inc(p_f_ready, 1)
                    fill(k, (2, 3))
                    next_keys(k, 2)

            run = body_loop(act, batch)
            with act.Fori(0, G) as g:
                act.wait_ge(stored, g * 16 + 16)
                act.dma_start(xg[0:TT, :, :], x[bass.ds(g * GT, GT), :].rearrange("(t p) n -> p t n", p=TT)
                              ).then_inc(x_in, 16)
                layer_norm(g * 2)
                for h in range(H):
                    act.wait_ge(q_full, g * H + h + 1)
                    nc.scalar.activation(q_all[:, :, 0, h * T:(h + 1) * T],
                                         banks[h % 4][:, 0:GT].rearrange("p (b t) -> p b t", b=GB), ACT.Copy,
                                         scale=1 / WS).then_inc(q_hi_ready, 1)
                b0 = g * GB
                for s in range(NSEG):
                    split_ct(b0, 0, True, s)
                    masks(b0, 0, s)
                split_c(b0, 0, True)
                run(g)
                for j in range(N_O):
                    out_turn((b0 + GB - 1, GB - 1), j, g * ((N_M + N_O) * GB) + (N_M + N_O) * GB - N_O + j + 1, j)
                for k in range(KD):
                    act.wait_ge(proj_full, g * KD + k + 1)
                    nc.scalar.activation(proj_t[:, k, :], banks[k][:, 0:GT], ACT.Copy).then_inc(proj_copied, 1)
                layer_norm(g * 2 + 1)
                act.wait_ge(logits_full, g + 1)
                nc.scalar.activation(r_exp[0:TT, :, :].rearrange("p t e -> p (t e)"), a_ps[0:TT, 0, 0:NT * E], ACT.Exp,
                                     scale=-1.0).then_inc(r_exp_ready, 1)
                for j in range(NH):
                    act.wait_ge(h_full, g * NH + j + 1)
                    if j >= 2:
                        act.wait_ge(h_step, (g * NH + j - 2) * 3 + 1)
                    nc.scalar.activation(s_f[:, j % 2, :], sc_ps[j % 2][:, 0, 0:GT], ACT.Silu, scale=1 / WS
                                         ).then_inc(silu_ready, 1)
                act.wait_ge(y_ready, (g + 1) * NT)
                act.dma_start(out[bass.ds(g * GT, GT), :].rearrange("(t p) n -> p t n", p=TT), xg[0:TT, :, :]
                              ).then_inc(stored, 16)
            act.wait_ge(stored, (G + 1) * 16)

        @block.vector
        def _(dve):
            dve.sem_inc(neg_ready, 1)
            nc.vector.memset(shift_m[:, :], 0.0).then_inc(zeroed_dve, 1)
            nc.vector.memset(neg_pad[:, :], 0.0).then_inc(zeroed_dve, 1)
            nc.vector.memset(nothing[:, 4:5], 0.0)
            nc.vector.memset(g_pad[:, :, :], 0.0).then_inc(zeroed_dve, 1)
            dve.wait_ge(zeroed_dve, 3)
            nc.vector.memset(g_pad[:, :, E:E + 1], 1.0).then_inc(zeroed_dve, 1)
            dve.wait_ge(th_ready, 1)
            nc.vector.tensor_scalar(gates[:, 0:1], gates_th[:, 0:1], 1 / NS, None, ALU.mult).then_inc(gates_ready, 1)
            nc.vector.tensor_scalar(gates[:, 1:2], gates_th[:, 1:2], 1 / WS, None, ALU.mult).then_inc(gates_ready, 1)
            for n in range(N_MIX):
                (hi, lo), scale = mix_out(n)
                dve.wait_ge(mix_hi, n + 1)
                nc.vector.scalar_tensor_tensor(lo, mix_ps(n), scale, hi, ALU.mult, ALU.subtract
                                               ).then_inc(mix_used, 1)
            nc.vector.memset(w2_f[HLAST:128, NH - 1, :], 0.0).then_inc(zeroed_w2, 1)
            for n, (w, f) in enumerate(((w1_hl, w1_f), (w3_hl, w3_f))):
                dve.wait_ge(w_hi, n + 1)
                nc.vector.scalar_tensor_tensor(w[1][:, :, 0:HID], f, WS, w[0][:, :, 0:HID], ALU.mult, ALU.subtract
                                               ).then_inc(w_ready, 1)
            dve.wait_ge(w_hi, 3)
            nc.vector.scalar_tensor_tensor(w2_hl[1][:, :, :], w2_f, WS, w2_hl[0][:, :, :], ALU.mult, ALU.subtract
                                           ).then_inc(w_ready, 1)
            dve.wait_ge(gates_ready, 2)
            dve.wait_ge(zeroed_dve, 4)
            dve.wait_ge(consts_in, 16 * N_CONSTS)

            def carry_wait(column):
                nc.vector.tensor_copy(nothing[:, column:column + 1], nothing[:, 4:5])

            def layer_norm(n):
                for t in range(NT):
                    s = nc.vector.bn_stats(stats[0:TT, t, :], xg[0:TT, t, :])
                s.then_inc(ln_step, 1)
                dve.wait_ge(ln_step, n * 3 + 1)
                carry_wait(3)
                for t in range(NT):
                    s = nc.vector.bn_aggr(mv[0:TT, t, :], stats[0:TT, t, :])
                s.then_inc(ln_step, 1)
                dve.wait_ge(ln_step, n * 3 + 2)
                nc.vector.tensor_scalar(var_eps[0:TT, :], mv[0:TT, :, 1], EPS, None, ALU.add).then_inc(ln_step, 1)
                dve.wait_ge(ln_sd, n + 1)
                nc.vector.reciprocal(rstd[0:TT, :], sd[0:TT, :]).then_inc(ln_rstd, 1)
                dve.wait_ge(ln_rstd, n + 1)
                for t in range(NT):
                    nc.vector.tensor_scalar(xn[0:TT, t, :], xg[0:TT, t, :], mv[0:TT, t, 0:1], rstd[0:TT, t:t + 1],
                                            ALU.subtract, ALU.mult).then_inc(xn_ready, 1)
                for k in range(KD):
                    dve.wait_ge(xt_hi_ready, n * KD + k + 1)
                    nc.vector.tensor_tensor(xt_hl[1][:, k, :], o_ps[:, k, 0:GT], xt_hl[0][:, k, :], ALU.subtract
                                            ).then_inc(xt_ready, 1)

            def seg(b, n, turn, a):
                s, j = n // NQ, n % NQ
                if j == 0:
                    dve.wait_ge(mask_ready, b * NSEG + s + 1)
                    carry_wait(2)
                dve.wait_ge(a_full, turn)
                carry_wait(a)
                nc.vector.tensor_tensor_reduce(max_junk[a], a_ps[:, a, 0:SEG], mask_b[:, s * SEG:(s + 1) * SEG],
                                               1.0, -3e38, ALU.add, ALU.max, maxes[:, j, s:s + 1]
                                               ).then_inc(a_used, 1)
                return j, s

            def negate(b, turn):
                dve.wait_ge(a_used, turn)
                nc.vector.tensor_reduce(neg_max[:, :], maxes[:, :, :], AX.X, ALU.max, negate=True).then_inc(dve_m, 1)
                dve.wait_ge(dve_m, m_of(b) + 1)
                for at in (0, LOW):
                    s = nc.vector.tensor_scalar(neg_pad[:, at:at + NQ], neg_max[:, :], 1e28, None, ALU.min)
                s.then_inc(neg_ready, 1)

            def row(b, u, j, turn, a):
                lo, hi = (0, 512) if j == 0 else (512, Q)
                dve.wait_ge(a_full, turn)
                nc.vector.tensor_copy(shift_b[:, u, lo:hi], a_ps[:, a, 0:hi - lo]).then_inc(a_used, 1)

            def shift(b, turn, a):
                dve.wait_ge(a_full, turn)
                nc.vector.tensor_copy(max_hi[:, :], a_ps[0:64, a, 0:128]).then_inc(dve_m, 1)
                dve.wait_ge(dve_m, m_of(b) + 2)
                nc.vector.scalar_tensor_tensor(shift_m[0:64, :], max_hi[:, :], low_rows[:, 0:1], a_ps[0:64, a, 0:128],
                                               ALU.mult, ALU.add).then_inc(a_used, 1)

            def normalise(b):
                dve.wait_ge(summed, b * NC + NC)
                six = o_ps[:, 0:2, 0:3 * VC].rearrange("p a (j n) -> p a j n", j=3)
                one = [o_ps[:, 0, 3 * VC:], o_ps[:, 1, 3 * VC:3 * VC + VC - CUT]]
                nc.vector.tensor_scalar(den[:, 0:6].rearrange("p (a j) -> p a j", a=2), six[:, :, :, DV], 1e-30, None,
                                        ALU.max)
                nc.vector.tensor_scalar(den[:, 6:7], one[1][:, DV - CUT:VC - CUT], 1e-30, None, ALU.max).then_inc(dve_o, 1)
                dve.wait_ge(dve_o, b * 2 + 1)
                nc.vector.reciprocal(rden[:, :], den[:, :]).then_inc(dve_o, 1)
                dve.wait_ge(dve_o, b * 2 + 2)
                for a in range(2):
                    nc.vector.tensor_tensor(o_f[:, 3 * a:3 * a + 3, :], six[:, a, :, 0:DV],
                                            rden[:, 3 * a:3 * a + 3].unsqueeze(2).broadcast_to([128, 3, DV]), ALU.mult)
                nc.vector.tensor_scalar(o_f[:, 6, 0:CUT], one[0], rden[:, 6:7], None, ALU.mult)
                nc.vector.tensor_scalar(o_f[:, 6, CUT:DV], one[1][:, 0:DV - CUT], rden[:, 6:7], None, ALU.mult
                                        ).then_inc(o_ready, 1)

            def out_turn(b, i, j, a):
                lo, hi = (0, 512) if j == 0 else (512, Q)
                dve.wait_ge(ot_hi, b * N_O + j + 1)
                nc.vector.tensor_tensor(q_all[:, bass.ds(i, 1), 1, lo:hi].rearrange("p b q -> p (b q)"),
                                        a_ps[:, a, 0:hi - lo],
                                        q_all[:, bass.ds(i, 1), 0, lo:hi].rearrange("p b q -> p (b q)"),
                                        ALU.subtract).then_inc(a_used, 1)

            def add_shift(b, k, u, turns):
                dve.wait_ge(scored, b * NC + k + 2)
                if k == 0:
                    dve.wait_ge(a_used, turns)
                halves = sc_ps[k % 2][0:SP, :, 0:HALF]
                nc.vector.scalar_tensor_tensor(halves, halves, mask_c[0:SP, u, k:k + 1],
                                               shift_b[0:SP, u, :].rearrange("p (a n) -> p a n", a=2),
                                               ALU.add, ALU.add).then_inc(shifted, 1)

            def take(kind, j, g, i, u, base, n):
                b, turn, a = g * GB + i, base + n, (n - 1) % 2
                if kind == "seg":
                    seg(b + 1, j, turn, a)
                    if j == N_SEG - 1:
                        negate(b + 1, turn)
                elif kind == "max":
                    shift(b + 1, turn, a)
                elif kind == "row":
                    row(b + 1, 1 - u, j, turn, a)
                elif kind == "out":
                    out_turn(b - 1, i - 1, j, a)

            def batch(g, i, u, v, first, last):
                b = g * GB + i
                plan = turn_plan(not last, not first)
                turn, base = 0, turns_before(g, i)
                for k in range(NC):
                    for slot in range(4):
                        if slot == 1:
                            if k == LAG - 1 and not first:
                                normalise(b - 1)
                            add_shift(b, k, u, base)
                        for kind, j in plan[k][slot]:
                            turn += 1
                            take(kind, j, g, i, u, base, turn)

            run = body_loop(dve, batch)
            with dve.Fori(0, G) as g:
                dve.wait_ge(x_in, g * 16 + 16)
                layer_norm(g * 2)
                for h in range(H):
                    dve.wait_ge(q_hi_ready, g * H + h + 1)
                    at = slice(h * T, (h + 1) * T)
                    nc.vector.scalar_tensor_tensor(q_all[:, :, 1, at],
                                                   banks[h % 4][:, 0:GT].rearrange("p (b t) -> p b t", b=GB), 1 / WS,
                                                   q_all[:, :, 0, at], ALU.mult, ALU.subtract).then_inc(q_ready, 1)
                b0 = g * GB
                turn0 = g * ((N_M + N_O) * GB)
                for n, (kind, j) in enumerate(PROLOGUE):
                    take(kind, j, g, -1, 1, turn0, n + 1)
                run(g)
                normalise(b0 + GB - 1)
                for j in range(N_O):
                    out_turn(b0 + GB - 1, GB - 1, j, j)
                for t in range(NT):
                    if t == 0:
                        dve.wait_ge(proj_back, g * KD + KD)
                    nc.vector.scalar_tensor_tensor(xg[0:TT, t, :], banks[2 + t // 2][0:TT, (t % 2) * D:(t % 2 + 1) * D],
                                                   gates[0:TT, 0:1],
                                                   xg[0:TT, t, :], ALU.mult, ALU.add).then_inc(x2_ready, 1)
                dve.wait_ge(x2_ready, g * NT + NT)
                layer_norm(g * 2 + 1)

                r0 = g * 11

                def step(ins, n):
                    ins.then_inc(r_step, 1)
                    dve.wait_ge(r_step, r0 + n)
                flat = "p t e -> p (t e)"
                dve.wait_ge(r_exp_ready, g + 1)
                step(nc.vector.tensor_scalar(r_one[0:TT, :, :], r_exp[0:TT, :, :], 1.0, None, ALU.add), 1)
                step(nc.vector.reciprocal(score[0:TT, :, :], r_one[0:TT, :, :]), 2)
                step(nc.vector.tensor_tensor(sel[0:TT, :, :], score[0:TT, :, :],
                                             bias_sb[0:TT, :].unsqueeze(1).broadcast_to([TT, NT, E]), ALU.add), 3)
                for t in range(NT):
                    other = sel[0:TT, t, :].unsqueeze(1).broadcast_to([TT, E, E])
                    own = sel[0:TT, t, :].unsqueeze(2).broadcast_to([TT, E, E])
                    nc.vector.tensor_tensor(ahead[0:TT, t, :, :], other, own, ALU.is_gt)
                    s = nc.vector.tensor_tensor(tied[0:TT, t, :, :], other, own, ALU.is_equal)
                step(s, 4)
                step(nc.vector.tensor_tensor(tied[0:TT, :, :, :].rearrange("p t e f -> p t (e f)"),
                                             tied[0:TT, :, :, :].rearrange("p t e f -> p t (e f)"),
                                             before_sb[0:TT, :].unsqueeze(1).broadcast_to([TT, NT, E * E]),
                                             ALU.mult), 5)
                step(nc.vector.tensor_tensor(ahead[0:TT, :, :, :], ahead[0:TT, :, :, :], tied[0:TT, :, :, :],
                                             ALU.add), 6)
                step(nc.vector.tensor_reduce(rank[0:TT, :, :], ahead[0:TT, :, :, :], AX.X, ALU.add), 7)
                step(nc.vector.scalar_tensor_tensor(w_top[0:TT, :, :], rank[0:TT, :, :], TOPK - 0.5,
                                                    score[0:TT, :, :], ALU.is_lt, ALU.mult), 8)
                step(nc.vector.tensor_reduce(w_sum[0:TT, :], w_top[0:TT, :, :], AX.X, ALU.add), 9)
                step(nc.vector.tensor_scalar(w_sum[0:TT, :], w_sum[0:TT, :], 1e-12, None, ALU.max), 10)
                step(nc.vector.reciprocal(w_rec[0:TT, :], w_sum[0:TT, :]), 11)
                for at in (0, LOW):
                    s = nc.vector.tensor_tensor(g_pad[0:TT, :, at:at + E], w_top[0:TT, :, :],
                                                w_rec[0:TT, :].unsqueeze(2).broadcast_to([TT, NT, E]), ALU.mult)
                s.then_inc(gate_ready, 1)
                dve.wait_ge(g_full, g + 1)
                nc.vector.tensor_copy(g_hi[:, :], a_ps[0:64, 0, 0:GT]).then_inc(g_ready, 1)
                dve.wait_ge(g_ready, g * 2 + 1)
                nc.vector.scalar_tensor_tensor(g_t[0:64, :], g_hi[:, :], low_rows[:, 0:1], a_ps[0:64, 0, 0:GT],
                                               ALU.mult, ALU.add).then_inc(g_ready, 1)
                for j in range(NH):
                    n = g * NH + j
                    dve.wait_ge(silu_ready, n + 1)
                    if j >= 2:
                        dve.wait_ge(h_used, n - 1)
                    nc.vector.tensor_tensor(v_f[:, 0, :], sc_ps[j % 2][:, 1, 0:GT], s_f[:, j % 2, :], ALU.mult
                                            ).then_inc(h_step, 1)
                    dve.wait_ge(h_step, n * 3 + 1)
                    nc.vector.scalar_tensor_tensor(v_f[:, 1, :], v_f[:, 0, :], 1 / WS, o_ps[:, j % 2, 0:GT],
                                                   ALU.mult, ALU.mult).then_inc(h_step, 1)
                    dve.wait_ge(h_step, n * 3 + 2)
                    nc.vector.tensor_copy(h_hl[:, j % 2, 0, 0:GT], v_f[:, 1, :]).then_inc(h_step, 1)
                    dve.wait_ge(h_step, n * 3 + 3)
                    nc.vector.tensor_tensor(h_hl[:, j % 2, 1, 0:GT], v_f[:, 1, :], h_hl[:, j % 2, 0, 0:GT],
                                            ALU.subtract).then_inc(h_ready, 1)
                dve.wait_ge(h_used, g * NH + NH)
                for t in range(NT):
                    acc = a_ps[0:TT, t // 2, (t % 2) * D:(t % 2 + 1) * D]
                    nc.vector.scalar_tensor_tensor(xg[0:TT, t, :], acc, gates[0:TT, 1:2], xg[0:TT, t, :],
                                                   ALU.mult, ALU.add).then_inc(y_ready, 1)

        @block.tensor
        def _(pe):
            def product(outs, lhs, rhs, first=True, last=True, **kw):
                mm = None
                for n, (a, c) in enumerate(((0, 0), (0, 1), (1, 0))):
                    mm = nc.tensor.matmul(outs, lhs[a], rhs[c], start=first and n == 0, stop=last and n == 2, **kw)
                return mm

            pe.sem_inc(scored, 1)
            pe.wait_ge(wq_in, 32)
            for n in range(N_MIX):
                h = n % H
                if n == H:
                    pe.wait_ge(wo_in, 32)
                if n >= 4:
                    pe.wait_ge(mix_used, n - 3)
                if n < H:
                    for k in range(KD):
                        mm = nc.tensor.matmul(mix_ps(n)[:, k, :], wq_f[:, h, k * 128:(k + 1) * 128],
                                              wk_f[:, h // 2, :], start=True, stop=True)
                else:
                    mm = nc.tensor.matmul(mix_ps(n), wv_f[:, h // 2, :], wo_f[:, h, :], start=True, stop=True)
                mm.then_inc(mix_made, 1)
            pe.wait_ge(w_ready, 3)
            pe.wait_ge(zeroed, N_ZERO)
            pe.wait_ge(consts_in, 16 * N_CONSTS)

            def layer_norm(n):
                pe.wait_ge(xn_ready, n * NT + NT)
                for k in range(KD):
                    for t in range(NT):
                        mm = nc.tensor.transpose(o_ps[:, k, t * TT:(t + 1) * TT], xn[0:TT, t, k * 128:(k + 1) * 128],
                                                 id_sb[0:TT, 0:TT])
                    mm.then_inc(xt_full, 1)
                pe.wait_ge(xt_ready, n * KD + KD)

            def take(kind, j, g, i, u, v, base, n, banks_free=False):
                b, a = g * GB + i, (n - 1) % 2
                if kind == "row" and j == 0:
                    pe.wait_ge(a_used, base + (n - 1))
                elif not banks_free:
                    pe.wait_ge(a_used, base + (n - 2))
                if kind == "seg":
                    s, t = j // NQ, j % NQ
                    if t == 0:
                        pe.wait_ge(ct_hi_ready, (b + 1) * NSEG + s + 1)
                    if j == 0:
                        pe.wait_ge(staged[1 - u], (v + u + 1) * 16)
                    mm = nc.tensor.matmul(a_ps[:, a, 0:SEG], q_st[:, 1 - u, 0, t * 128:(t + 1) * 128],
                                          ct[1 - u][0][:, s * SEG:(s + 1) * SEG], start=True, stop=True)
                elif kind == "row":
                    for t in (range(0, 4) if j == 0 else range(4, NQ)):
                        mm = nc.tensor.matmul(a_ps[:, a, (t % 4) * 128:(t % 4 + 1) * 128], pick_sb[:, t, :],
                                              shift_m[:, :], start=True, stop=True)
                elif kind == "max":
                    pe.wait_ge(neg_ready, b + 3)
                    mm = nc.tensor.transpose(a_ps[:, a, 0:128], neg_pad[:, :], id_sb[:, :])
                else:
                    if j == 0:
                        pe.wait_ge(o_ready, b)
                    for t in (range(0, 4) if j == 0 else range(4, NQ)):
                        mm = nc.tensor.transpose(a_ps[:, a, (t % 4) * 128:(t % 4 + 1) * 128], o_f[:, t, :], id_sb[:, :])
                mm.then_inc(a_full, 1)

            def scores(b, k, u, v, first, slot0):
                n = b * NC + k
                if not (first and k < 2):
                    pe.wait_ge(p_f_ready, n - 1)
                if k == 0:
                    pe.wait_ge(split_done, b * 2 + 2)
                keys_k = slice(k * SP, (k + 1) * SP)
                for n_pass, (kp, qp) in enumerate(((0, 0), (0, 1), (1, 0))):
                    for a in range(2):
                        mm = nc.tensor.matmul(sc_ps[k % 2][0:SP, a, 0:HALF], ct[u][kp][:, keys_k],
                                              q_st[:, u, qp, a * HALF:(a + 1) * HALF], start=n_pass == 0, stop=n_pass == 2)
                    if n_pass == 0:
                        slot0()
                mm.then_inc(scored, 1)

            def weighted(b, k, u, first, slot2):
                pe.wait_ge(p_ready, b * NC + k + 1)
                if k == 0:
                    pe.wait_ge(split_done, b * 2 + 3)
                    if not first:
                        pe.wait_ge(o_ready, b)
                hi, lo = p_hl[0:SP, k % NPB, 0, :], p_hl[0:SP, k % NPB, 1, :]
                for t in range(NQ):
                    q = slice(t * 128, (t + 1) * 128)
                    pieces = [(t // 3, (t % 3) * VC, 0, VC)] if t < 6 else [(0, 3 * VC, 0, CUT), (1, 3 * VC, CUT, VC)]
                    for n, (p, c, w) in enumerate(((hi, 0, VC), (hi, VC, DV), (lo, 0, VC))):
                        for bank, at, c0, c1 in pieces:
                            c1 = min(c1, w)
                            mm = nc.tensor.matmul(o_ps[:, bank, at:at + c1 - c0], p[:, q],
                                                  cv[u][0:SP, k, c + c0:c + c1],
                                                  start=k == 0 and t in (0, 3) and n == 0,
                                                  stop=k == NC - 1 and n == 2, skip_group_check=True)
                    if t == 3:
                        slot2()
                mm.then_inc(summed, 1)

            def batch(g, i, u, v, first, last):
                b = g * GB + i
                plan = turn_plan(not last, not first)
                base = turns_before(g, i)
                before = [0]

                def fill(k, slot):
                    for kind, j in plan[k][slot]:
                        before[0] += 1
                        take(kind, j, g, i, u, v, base, before[0])

                for k in range(NC):
                    if k == LAG - 1 and not first:
                        weighted(b - 1, NC - 1, 1 - u, False, lambda: None)
                    scores(b, k, u, v, first, lambda: fill(k, 0))
                    fill(k, 1)
                    if k >= LAG:
                        weighted(b, k - LAG, u, first, lambda: fill(k, 2))
                    elif k < LAG - 1 and not first:
                        weighted(b - 1, NC - LAG + k, 1 - u, False, lambda: fill(k, 2))
                    else:
                        fill(k, 2)
                    fill(k, 3)

            run = body_loop(pe, batch)
            with pe.Fori(0, G) as g:
                layer_norm(g * 2)
                for h in range(H):
                    if h >= 4:
                        pe.wait_ge(q_ready, g * H + h - 3)
                    for k in range(KD):
                        mm = product(banks[h % 4][:, 0:GT], [m[:, k, h, :] for m in m_hl],
                                     [xt[:, k, :] for xt in xt_hl], k == 0, k == KD - 1)
                    mm.then_inc(q_full, 1)
                b0 = g * GB
                turn0 = g * ((N_M + N_O) * GB)
                pe.wait_ge(q_ready, g * H + H)
                for n, (kind, j) in enumerate(PROLOGUE):
                    take(kind, j, g, -1, 1, g * (GB // 2) - 1, turn0, n + 1, banks_free=n < 2)
                run(g)
                for k in range(NC - LAG, NC):
                    weighted(b0 + GB - 1, k, 1, False, lambda: None)
                for j in range(N_O):
                    take("out", j, g, GB, 0, 0, turn0 + (N_M + N_O) * GB - N_O, j + 1)
                pe.wait_ge(a_used, turn0 + (N_M + N_O) * GB)
                for k in range(KD):
                    for h in range(H):
                        ot = [q_all[:, :, p, h * T:(h + 1) * T] for p in range(2)]
                        mm = product(banks[k][:, 0:GT], [n_[:, h, k * 128:(k + 1) * 128] for n_ in n_hl], ot,
                                     h == 0, h == H - 1)
                    mm.then_inc(proj_full, 1)
                for k in range(KD):
                    pe.wait_ge(proj_copied, g * KD + k + 1)
                    for t in range(NT):
                        mm = nc.tensor.transpose(banks[2 + t // 2][0:TT, (t % 2) * D + k * 128:(t % 2) * D + (k + 1) * 128],
                                                 proj_t[:, k, t * TT:(t + 1) * TT], id_sb[:, :])
                    mm.then_inc(proj_back, 1)
                layer_norm(g * 2 + 1)
                for t in range(NT):
                    for k in range(KD):
                        mm = nc.tensor.matmul(a_ps[0:TT, 0, t * E:(t + 1) * E], xt_f[:, k, t * TT:(t + 1) * TT],
                                              gate_sb[:, k, :], start=k == 0, stop=k == KD - 1)
                mm.then_inc(logits_full, 1)
                pe.wait_ge(gate_ready, g + 1)
                for t in range(NT):
                    mm = nc.tensor.transpose(a_ps[:, 0, t * TT:(t + 1) * TT], g_pad[0:TT, t, :], id_sb[0:TT, 0:TT])
                mm.then_inc(g_full, 1)
                pe.wait_ge(g_ready, g * 2 + 2)

                def down(j):
                    pe.wait_ge(h_ready, g * NH + j + 1)
                    for t in range(NT):
                        acc = a_ps[0:TT, t // 2, (t % 2) * D:(t % 2 + 1) * D]
                        hid = [h_hl[:, j % 2, p, t * TT:(t + 1) * TT] for p in range(2)]
                        mm = product(acc, hid, [w[:, j, :] for w in w2_hl], j == 0 and t % 2 == 0, j == NH - 1,
                                     skip_group_check=True)
                    mm.then_inc(h_used, 1)

                for j in range(NH):
                    if j >= 2:
                        pe.wait_ge(h_ready, g * NH + j - 1)
                    hid = slice(j * 128, (j + 1) * 128)
                    for a, w in enumerate((w1_hl, w3_hl)):
                        for k in range(KD):
                            product(sc_ps[j % 2][:, a, 0:GT], [p[:, k, hid] for p in w], [xt[:, k, :] for xt in xt_hl],
                                    k == 0, k == KD - 1)
                    nc.tensor.matmul(o_ps[:, j % 2, 0:GT], expand_sb[:, hid], g_t[:, :], start=True, stop=True
                                     ).then_inc(h_full, 1)
                    if j >= 1:
                        down(j - 1)
                down(NH - 1)
                pe.wait_ge(y_ready, g * NT + NT)


def kernel(x, ctx_1024, mask_BxS2_bf1, g_xattn, g_ffn, L0_xattn_Wq, L0_xattn_Wk, L0_xattn_Wv, L0_xattn_Wo,
           L0_ffn_gate_w, L0_ffn_router_bias, L0_ffn_W1, L0_ffn_W3, L0_ffn_W2, L0_ffn_sw1, L0_ffn_sw3, L0_ffn_sw2):
    import numpy as np
    import concourse.bacc as bacc
    from concourse import mybir as mb
    from concourse.bass_utils import run_bass_kernel_spmd as launch

    def lay(a):
        return np.ascontiguousarray(a)

    ctx_h = np.asarray(ctx_1024)
    mask_h = np.asarray(mask_BxS2_bf1).view(np.uint8)
    pick = np.zeros((128, NQ, 128), mb.dt.np(BF16))
    for j in range(NQ):
        pick[j, j], pick[LOW + j, j] = 1, 1
    expand = np.zeros((128, NH * 128), np.float16)
    for j in range(HID):
        e = min(j // INTER, E)
        expand[e, j] = 1
        if e < E:
            expand[LOW + e, j] = 1
    before = np.zeros((128, E * E), np.float32)
    for e in range(E):
        before[:, e * E:e * E + e] = 1
    low = np.zeros((64, 1), np.float32)
    low[LOW:] = -1
    w1, w3, w2 = np.asarray(L0_ffn_W1), np.asarray(L0_ffn_W3), np.asarray(L0_ffn_W2)
    arrays = {
        "x": lay(np.asarray(x).reshape(B * T, D)),
        "ctx": lay(ctx_h),
        "ctxT": lay(ctx_h.reshape(B, SP, NC, DV).transpose(0, 3, 2, 1).reshape(B, DV, S)),
        "mask": lay(mask_h),
        "maskT": lay(mask_h.reshape(B, SP, NC).transpose(0, 2, 1).reshape(B, S)),
        "g_xattn": lay(g_xattn), "g_ffn": lay(g_ffn),
        "wqT": lay(np.asarray(L0_xattn_Wq).T.reshape(H, DH, D)),
        "wkT": lay(np.asarray(L0_xattn_Wk).T.reshape(KV, DH, DV)),
        "wvT": lay(np.asarray(L0_xattn_Wv).T.reshape(KV, DH, DV)),
        "wo": lay(np.asarray(L0_xattn_Wo).reshape(H, DH, D)),
        "gateT": lay(np.asarray(L0_ffn_gate_w).T),
        "rbias": lay(L0_ffn_router_bias),
        "w1": lay(np.concatenate([w1.transpose(1, 0, 2).reshape(D, E * INTER), np.asarray(L0_ffn_sw1).T], 1)),
        "w3": lay(np.concatenate([w3.transpose(1, 0, 2).reshape(D, E * INTER), np.asarray(L0_ffn_sw3).T], 1)),
        "w2": lay(np.concatenate([w2.reshape(E * INTER, D), np.asarray(L0_ffn_sw2).T], 0)),
        "ident": np.eye(128, dtype=np.float32), "pick": pick, "expand": expand, "before": before, "low": low,
    }
    nc = bacc.Bacc("TRN2", target_bir_lowering=False, num_devices=1)
    aps = {n: nc.dram_tensor(f"in_{n}", a.shape, mb.dt.from_np(a.dtype), kind="ExternalInput").ap()
           for n, a in arrays.items()}
    out = nc.dram_tensor("out", (B * T, D), F32, kind="ExternalOutput").ap()
    build(nc, **aps, out=out)
    r = launch(nc, [{f"in_{n}": a for n, a in arrays.items()}], core_ids=[0])
    return r.results[0]["out"].reshape(B, T, D)
```

```python
from contextlib import ExitStack

import concourse.bass as bass
from concourse import mybir

F32, F16, BF16, U8 = mybir.dt.float32, mybir.dt.float16, mybir.dt.bfloat16, mybir.dt.uint8
ACT = mybir.ActivationFunctionType
ALU = mybir.AluOpType
AX = mybir.AxisListType

B, T, D = 32, 56, 256
S, DV = 1500, 128
H, KV, DH = 16, 8, 128
E, TOPK, INTER, NSH = 8, 2, 176, 352
NC = 12
SP = S // NC
Q = H * T
NQ = Q // 128
HALF = Q // 2
NSEG, SEG = 3, S // 3
GB = 8
G = B // GB
GT = GB * T
NT, TT = 4, GT // 4
KD = D // 128
HID = E * INTER + NSH
NH = -(-HID // 128)
HLAST = HID - (NH - 1) * 128
VC = DV + 1
CUT = 512 - 3 * VC
EPS = 1e-5
MASKED = -1e30
WS = 64.0
NS = 256.0
LOW = 32
NPB = 4
LAG = 3

SEG_SLOTS = [(), (2, 3), (0, 2), (2, 3), (0, 3), (0, 2), (0, 2, 3), (0, 2), (0, 2), (0, 2, 3), (0,), ()]
OUT_SLOTS, MAX_SLOT, ROW_SLOTS = ((4, 1), (5, 1)), (11, 0), ((11, 2), (11, 3))
KEY_STEPS = {(0, 0): ("ct", 0), (0, 2): ("mask", 0), (1, 2): ("ct", 1), (3, 2): ("mask", 1), (4, 2): ("ct", 2),
             (5, 2): ("mask", 2), (6, 2): ("c", 0)}
EARLY = [("ct", 0), ("mask", 0), ("ct", 1)]
POOL_CT, POOL_C = 5, 7
N_SEG = NQ * NSEG
N_M, N_O = N_SEG + 1 + len(ROW_SLOTS), len(OUT_SLOTS)


FIRST = [("seg", j) for j in range(N_SEG)] + [("max", 0), ("row", 0), ("row", 1)]
TURNS_AROUND = [(1, 0), (0, 1)] + [(1, 1)] * 11 + [(0, 0)] * (NH - 13)
assert sum(a + b for a, b in TURNS_AROUND) == N_M


def turn_plan(has_next, has_last):
    plan, n = [[[] for _ in range(4)] for _ in range(NC)], 0
    for k in range(NC):
        for slot in SEG_SLOTS[k] if has_next else ():
            plan[k][slot].append(("seg", n))
            n += 1
    assert n == (N_SEG if has_next else 0)
    if has_next:
        plan[MAX_SLOT[0]][MAX_SLOT[1]].append(("max", 0))
        for j, (k, slot) in enumerate(ROW_SLOTS):
            plan[k][slot].append(("row", j))
    if has_last:
        for j, (k, slot) in enumerate(OUT_SLOTS):
            plan[k][slot].append(("out", j))
    return plan


def build(nc, x, ctx, ctxT, mask, maskT, g_xattn, g_ffn, wqT, wkT, wvT, wo, gateT, rbias, w1, w3, w2, ident, pick,
          expand, before, low, out):
    with ExitStack() as stack:
        def sb(name, shape, dt):
            return stack.enter_context(nc.sbuf_tensor(name, shape, dt))

        def ps(name, shape, dt):
            return stack.enter_context(nc.psum_tensor(name, shape, dt))

        def sem(name):
            return stack.enter_context(nc.semaphore(name))

        sc_ps = [ps(f"sc_ps{i}", [128, 2, 512], F32) for i in range(2)]
        o_ps = ps("o_ps", [128, 2, 512], F32)
        a_ps = ps("a_ps", [128, 2, 512], F32)

        m_hl = [sb(f"m_{p}", [128, KD, H, 128], F16) for p in ("hi", "lo")]
        n_hl = [sb(f"n_{p}", [128, H, D], F16) for p in ("hi", "lo")]
        w1_hl = [sb(f"w1_{p}", [128, KD, NH * 128], F16) for p in ("hi", "lo")]
        w3_hl = [sb(f"w3_{p}", [128, KD, NH * 128], F16) for p in ("hi", "lo")]
        w2_both = sb("w2_both", [128, 2, NH, D], F16)
        w2_hl = [w2_both[:, p, :, :] for p in range(2)]
        gate_sb = sb("gate_sb", [128, KD, E], F32)
        bias_sb = sb("bias_sb", [128, E], F32)
        id_sb = sb("id_sb", [128, 128], F32)
        pick_sb = sb("pick_sb", [128, NQ, 128], BF16)
        expand_sb = sb("expand_sb", [128, NH * 128], F16)
        before_sb = sb("before_sb", [128, E * E], F32)
        gates_in = sb("gates_in", [128, 2], F32)
        gates_th = sb("gates_th", [128, 2], F32)
        gates = sb("gates", [128, 2], F32)
        nothing = sb("nothing", [128, 5], F32)
        low_rows = sb("low_rows", [64, 1], F32)

        q_all = sb("q_all", [128, GB, 2, Q], F16)
        q_st = sb("q_st", [128, 2, 2, Q], F16)

        c_f = sb("c_f", [128, NC, DV], F32)
        ct_f = sb("ct_f", [128, S], F32)
        mask_u8 = sb("mask_u8", [128, S], U8)
        keys = sb("keys", [128, 2, 2 * S + NC * (VC + DV)], F16)
        ct = [[keys[:, u, p * S:(p + 1) * S] for p in range(2)] for u in range(2)]
        cv = [keys[:, u, 2 * S:].rearrange("p (c n) -> p c n", c=NC) for u in range(2)]
        mask_n = sb("mask_n", [128, NC], U8)
        mask_b = sb("mask_b", [128, S], BF16)
        mask_c = sb("mask_c", [128, 2, NC], F32)
        shift_m = sb("shift_m", [128, 128], BF16)
        shift_b = sb("shift_b", [128, 2, Q], F32)

        p_f = sb("p_f", [128, 2, Q], F32)
        p_hl = sb("p_hl", [128, NPB, 2, Q], F16)
        h_hl = p_hl
        s_f = p_f[:, 0, :].rearrange("p (u n) -> p u n", u=2)
        v_f = p_f[:, 1, :].rearrange("p (u n) -> p u n", u=2)
        maxes = sb("maxes", [128, NQ, NSEG], F32)
        neg_max = sb("neg_max", [128, NQ], F32)
        neg_pad = sb("neg_pad", [128, 128], F32)
        max_hi = sb("max_hi", [64, 128], BF16)
        den = sb("den", [128, NQ], F32)
        rden = sb("rden", [128, NQ], F32)
        o_f = sb("o_f", [128, NQ, DV], F32)

        xg = sb("xg", [128, NT, D], F32)
        xn = sb("xn", [128, NT, D], F32)
        max_junk = [xn[:, 2 * a:2 * a + 2, :].rearrange("p t d -> p (t d)")[:, 0:SEG] for a in range(2)]
        xt_f = o_f[:, :, :].rearrange("p j d -> p (j d)").rearrange("p (k n) -> p k n", k=KD)
        xt_hl = [sb(f"xt_{p}", [128, KD, GT], F16) for p in ("hi", "lo")]
        x_next = p_f[:, :, :].rearrange("p u n -> p (u n)")[:, 0:NT * D].rearrange("p (t n) -> p t n", t=NT)
        xt_next_hl = [p_hl[:, 0, p, :].rearrange("p (k n) -> p k n", k=KD) for p in range(2)]
        proj_t = xt_f
        stats = sb("stats", [128, NT, 6], F32)
        mv = sb("mv", [128, NT, 2], F32)
        var_eps = sb("var_eps", [128, NT], F32)
        sd = sb("sd", [128, NT], F32)
        rstd = sb("rstd", [128, NT], F32)
        r_exp = sb("r_exp", [128, NT, E], F32)
        r_one = sb("r_one", [128, NT, E], F32)
        score = sb("score", [128, NT, E], F32)
        sel = sb("sel", [128, NT, E], F32)
        ahead, tied = [xn[:, a, :].rearrange("p (t e f) -> p t e f", t=NT, e=E) for a in range(2)]
        rank = sb("rank", [128, NT, E], F32)
        w_top = sb("w_top", [128, NT, E], F32)
        w_sum = sb("w_sum", [128, NT], F32)
        w_rec = sb("w_rec", [128, NT], F32)
        g_pad = sb("g_pad", [128, NT, 128], F32)
        g_hi = sb("g_hi", [64, GT], F16)
        g_t = sb("g_t", [128, GT], F16)

        id_in = sem("id_in")
        consts_in = sem("consts_in")
        late_consts_in = sem("late_consts_in")
        wk_in = sem("wk_in")
        wq_in = [sem(f"wq_in{i}") for i in range(2)]
        wv_in = sem("wv_in")
        wo_in = [sem(f"wo_in{i}") for i in range(2)]
        w1_in = sem("w1_in")
        w3_in = sem("w3_in")
        w2_in = sem("w2_in")
        zeroed = sem("zeroed")
        zeroed_dve = sem("zeroed_dve")
        zeroed_w2 = sem("zeroed_w2")
        mix_made = sem("mix_made")
        mix_hi = sem("mix_hi")
        mix_used = sem("mix_used")
        w1_hi = sem("w1_hi")
        w1_ready = sem("w1_ready")
        w3_scaled = sem("w3_scaled")
        w3_hi = sem("w3_hi")
        w3_ready = sem("w3_ready")
        w2_scaled = sem("w2_scaled")
        w2_hi = sem("w2_hi")
        w2_ready = sem("w2_ready")
        th_ready = sem("th_ready")
        gates_ready = sem("gates_ready")

        ctx_in = sem("ctx_in")
        staged = [sem(f"staged{u}") for u in range(2)]
        mask_ready = sem("mask_ready")
        ct_hi_ready = sem("ct_hi_ready")
        c_hi_ready = sem("c_hi_ready")
        split_done = sem("split_done")
        scored = sem("scored")
        shifted = sem("shifted")
        p_hi_ready = sem("p_hi_ready")
        p_f_ready = sem("p_f_ready")
        p_ready = sem("p_ready")
        summed = sem("summed")
        a_full = sem("a_full")
        a_used = sem("a_used")
        neg_ready = sem("neg_ready")
        o_ready = sem("o_ready")
        o_act = sem("o_act")
        ot_hi = sem("ot_hi")
        dve_m = sem("dve_m")
        dve_o = sem("dve_o")

        x_next_in = sem("x_next_in")
        x_in = sem("x_in")
        ln_step = sem("ln_step")
        ln_sd = sem("ln_sd")
        ln_rstd = sem("ln_rstd")
        xn_ready = sem("xn_ready")
        xt_full = sem("xt_full")
        xt_hi_ready = sem("xt_hi_ready")
        xt_ready = sem("xt_ready")
        q_full = sem("q_full")
        q_hi_ready = sem("q_hi_ready")
        q_ready = sem("q_ready")
        proj_full = sem("proj_full")
        proj_copied = sem("proj_copied")
        proj_back = sem("proj_back")
        x2_ready = sem("x2_ready")
        logits_full = sem("logits_full")
        r_exp_ready = sem("r_exp_ready")
        r_step = sem("r_step")
        gate_ready = sem("gate_ready")
        g_full = sem("g_full")
        g_ready = sem("g_ready")
        h_full = sem("h_full")
        e_full = sem("e_full")
        silu_ready = sem("silu_ready")
        h_step = sem("h_step")
        h_ready = sem("h_ready")
        h_used = sem("h_used")
        y_ready = sem("y_ready")
        stored = sem("stored")

        room1 = q_all[:].rearrange("p b u q -> p (b u q)").bitcast(F32)
        room2 = keys[:].rearrange("p u n -> p (u n)").bitcast(F32)
        room3 = w2_both[:].rearrange("p u t n -> p (u t n)").bitcast(F32)
        room4 = p_hl[:].rearrange("p u v q -> p (u v q)").bitcast(F32)
        wq_f = room1[:, 0:H * D].rearrange("p (h n) -> p h n", h=H)
        wk_f = room1[:, H * D:H * D + KV * DV].rearrange("p (h n) -> p h n", h=KV)
        wo_f = room2[:, 0:H * D].rearrange("p (h n) -> p h n", h=H)
        wv_f = room2[:, H * D:H * D + KV * DV].rearrange("p (h n) -> p h n", h=KV)
        w1_f = room3[:, 0:KD * HID].rearrange("p (k n) -> p k n", k=KD)
        w3_f = room4[:, 0:KD * HID].rearrange("p (k n) -> p k n", k=KD)
        NHA = 11
        w2_f = [keys[:, 1, :].bitcast(F32)[:, 0:NHA * D].rearrange("p (t n) -> p t n", t=NHA),
                o_f[:].rearrange("p j d -> p (j d)")[:, 0:(NH - NHA) * D].rearrange("p (t n) -> p t n", t=NH - NHA)]
        w2_parts = [(w2_f[0], slice(0, NHA)), (w2_f[1], slice(NHA, NH))]
        banks = [sc_ps[0][:, 0, :], sc_ps[0][:, 1, :], sc_ps[1][:, 0, :], sc_ps[1][:, 1, :]]

        ROOT_AT, TURN_X_AT, LOGITS_AT, ROUTER_AT = 2, 7, 11, 14
        W1_AT, W3_AT = 3, (8, 12)
        a_banks = [a_ps[:, 0, :], a_ps[:, 1, :]]
        ffn_bank = [o_ps[:, 1, :]]

        N_CONSTS = 4
        N_ZERO = 7
        N_MIX = 2 * H

        def mix_out(n):
            h = n % H
            return [(m_hl[p][:, :, h, :] if n < H else n_hl[p][:, h, :]) for p in range(2)], \
                (WS / DH ** 0.5 if n < H else NS)

        def mix_ps(n):
            b = banks[n % 4][:, 0:2 * 128]
            return b.rearrange("p (k n) -> p k n", k=KD) if n < H else b

        def turns_before(g, i):
            return g * ((N_M + N_O) * GB) + (i * (N_M + N_O) + (N_M if isinstance(i, int) and i == 0 else N_M - N_O))

        STEPS_M = 2

        def ln_of(g, has_next):
            return g * 2 + 1, g * 2 + (2 if has_next else 1)

        def all_groups(eng, group):
            with eng.Fori(0, G - 1) as g:
                group(g, True)
            group(G - 1, False)

        def m_of(b):
            return b * STEPS_M

        def body_loop(eng, per_batch):
            def run(g):
                half = g * (GB // 2)
                per_batch(g, 0, 0, half, True, False)
                with eng.Fori(0, (GB - 2) // 2) as r:
                    per_batch(g, r * 2 + 1, 1, half + r, False, False)
                    per_batch(g, r * 2 + 2, 0, half + r + 1, False, False)
                per_batch(g, GB - 1, 1, half + (GB // 2 - 1), False, True)
            return run

        block = stack.enter_context(nc.Block())


        @block.sync
        def _(sp):
            sp.dma_start(wk_f, wkT.rearrange("h e n -> e h n")).then_inc(wk_in, 16)
            for part in range(2):
                heads = slice(part * (H // 2), (part + 1) * (H // 2))
                sp.dma_start(wq_f[:, heads, :], wqT[heads].rearrange("h e n -> e h n")).then_inc(wq_in[part], 16)
            sp.dma_start(wv_f, wvT.rearrange("h e n -> e h n")).then_inc(wv_in, 16)
            for part in range(2):
                heads = slice(part * (H // 2), (part + 1) * (H // 2))
                sp.dma_start(wo_f[:, heads, :], wo[heads].rearrange("h e n -> e h n")).then_inc(wo_in[part], 16)
            sp.dma_start(id_sb[:, :], ident).then_inc(id_in, 16)
            sp.dma_start(low_rows[:, :], low).then_inc(consts_in, 16)
            sp.dma_start(gates_in[:, 0:1], g_xattn.partition_broadcast(128)).then_inc(consts_in, 16)
            sp.dma_start(gates_in[:, 1:2], g_ffn.partition_broadcast(128)).then_inc(consts_in, 16)
            sp.dma_start(pick_sb[:, :, :], pick).then_inc(consts_in, 16)
            sp.dma_start(w1_f, w1.rearrange("(k p) n -> p k n", k=KD)).then_inc(w1_in, 16)
            sp.dma_start(w3_f, w3.rearrange("(k p) n -> p k n", k=KD)).then_inc(w3_in, 16)
            sp.wait_ge(mix_used, 2 * H)
            sp.dma_start(w2_f[0], w2[0:NHA * 128, :].rearrange("(t p) n -> p t n", p=128)).then_inc(w2_in, 16)
            sp.dma_start(w2_f[1][:, 0:NH - 1 - NHA, :], w2[NHA * 128:(NH - 1) * 128, :].rearrange("(t p) n -> p t n", p=128)
                         ).then_inc(w2_in, 16)
            sp.dma_start(w2_f[1][0:HLAST, NH - 1 - NHA, :], w2[(NH - 1) * 128:HID, :]).then_inc(w2_in, 16)
            sp.dma_start(expand_sb[:, :], expand).then_inc(late_consts_in, 16)
            sp.dma_start(before_sb[:, :], before).then_inc(late_consts_in, 16)
            sp.dma_start(gate_sb[:, :, :], gateT.rearrange("(k p) e -> p k e", k=KD)).then_inc(late_consts_in, 16)
            sp.dma_start(bias_sb[:, :], rbias.partition_broadcast(128)).then_inc(late_consts_in, 16)

            def batch(g, i, u, v, first, last):
                b = g * GB + i
                sp.wait_ge(split_done, b * 2 + 1)
                sp.dma_start(ct_f[:, :], ctxT[bass.ds(b, 1)].rearrange("b d s -> (b d) s")).then_inc(ctx_in, 16)
                sp.dma_start(mask_u8[:, :], maskT[bass.ds(b, 1), :].rearrange("b s -> (b s)").partition_broadcast(128)
                             ).then_inc(ctx_in, 16)
                sp.dma_start(mask_n[0:SP, :], mask[bass.ds(b, 1), :].rearrange("b (p c) -> (b p) c", c=NC)
                             ).then_inc(ctx_in, 16)
                sp.dma_start(c_f[0:SP, :, :], ctx[bass.ds(b, 1)].rearrange("b (p c) d -> (b p) c d", c=NC)
                             ).then_inc(ctx_in, 16)
                sp.wait_ge(q_ready, g * H + H)
                if not first:
                    sp.wait_ge(scored, b * NC - NC + 1)
                sp.dma_start(q_st[:, u, :, :], q_all[:, bass.ds(i, 1), :, :].rearrange("p b u q -> p (b u) q")
                             ).then_inc(staged[u], 16)

            run = body_loop(sp, batch)
            with sp.Fori(0, G) as g:
                run(g)

        @block.gpsimd
        def _(pool):
            pool.sem_inc(split_done, 1)
            nc.gpsimd.memset(w1_hl[0][:, :, HID:], 0.0).then_inc(zeroed, 1)
            nc.gpsimd.memset(w1_hl[1][:, :, HID:], 0.0).then_inc(zeroed, 1)
            nc.gpsimd.memset(w3_hl[0][:, :, HID:], 0.0).then_inc(zeroed, 1)
            nc.gpsimd.memset(w3_hl[1][:, :, HID:], 0.0).then_inc(zeroed, 1)
            nc.gpsimd.memset(g_t[:, :], 0.0).then_inc(zeroed, 1)
            pool.wait_ge(zeroed, 5)
            pool.wait_ge(mix_used, 2 * H)
            nc.gpsimd.memset(cv[0][:, :, DV:VC], 1.0).then_inc(zeroed, 1)
            pool.wait_ge(w3_hi, 1)
            nc.gpsimd.tensor_tensor(w3_hl[1][:, :, 0:HID], w3_f, w3_hl[0][:, :, 0:HID], ALU.subtract
                                    ).then_inc(w3_ready, 1)

            def split_ct(b, u):
                pool.wait_ge(ct_hi_ready, b * NSEG + NSEG)
                nc.gpsimd.tensor_tensor(ct[u][1], ct_f[:, :], ct[u][0], ALU.subtract).then_inc(split_done, 1)

            def split_c(b, u):
                pool.wait_ge(c_hi_ready, b + 1)
                nc.gpsimd.tensor_tensor(cv[u][0:SP, :, VC:], c_f[0:SP, :, :], cv[u][0:SP, :, 0:DV], ALU.subtract
                                        ).then_inc(split_done, 1)

            def batch(g, i, u, v, first, last):
                b = g * GB + i
                for k in range(NC):
                    pool.wait_ge(p_f_ready, b * NC + k + 1)
                    nc.gpsimd.tensor_tensor(p_hl[0:SP, k % NPB, 1, :], p_f[0:SP, k % 2, :], p_hl[0:SP, k % NPB, 0, :],
                                            ALU.subtract).then_inc(p_ready, 1)
                    if not last and k == POOL_CT:
                        split_ct(b + 1, 1 - u)
                    if not last and k == POOL_C:
                        split_c(b + 1, 1 - u)

            run = body_loop(pool, batch)
            def first_keys(b0):
                split_ct(b0, 0)
                split_c(b0, 0)

            def group(g, has_next):
                run(g)
                if has_next:
                    first_keys(g * GB + GB)

            first_keys(0)
            for n, (w_f, tiles) in enumerate(w2_parts):
                pool.wait_ge(w2_hi, n + 1)
                nc.gpsimd.tensor_tensor(w2_hl[1][:, tiles, :], w_f, w2_hl[0][:, tiles, :], ALU.subtract
                                        ).then_inc(w2_ready, 1)
            pool.wait_ge(w2_ready, 2)
            nc.gpsimd.memset(cv[1][:, :, DV:VC], 1.0).then_inc(zeroed, 1)
            pool.wait_ge(zeroed, N_ZERO)
            all_groups(pool, group)

        @block.scalar
        def _(act):
            act.sem_inc(stored, 16)
            def root(n):
                act.wait_ge(ln_step, n * 3 + 3)
                nc.scalar.activation(sd[0:TT, :], var_eps[0:TT, :], ACT.Sqrt).then_inc(ln_sd, 1)

            def split_x(n, keep_f, to=xt_hl):
                for k in range(KD):
                    act.wait_ge(xt_full, n * KD + k + 1)
                    if keep_f:
                        nc.scalar.activation(xt_f[:, k, :], o_ps[:, k, 0:GT], ACT.Copy)
                    nc.scalar.activation(to[0][:, k, :], o_ps[:, k, 0:GT], ACT.Copy).then_inc(xt_hi_ready, 1)

            def split_ct(b, u, first, s):
                if s == 0:
                    act.wait_ge(ctx_in, b * 64 + 64)
                    if not first:
                        act.wait_ge(scored, b * NC - NC + 1)
                at = slice(s * SEG, (s + 1) * SEG)
                nc.scalar.activation(ct[u][0][:, at], ct_f[:, at], ACT.Copy).then_inc(ct_hi_ready, 1)

            def split_c(b, u, first):
                if not first:
                    act.wait_ge(summed, b * NC - NC)
                nc.scalar.activation(cv[u][0:SP, :, 0:DV], c_f[0:SP, :, :], ACT.Copy).then_inc(c_hi_ready, 1)

            def masks(b, u, s):
                if s == 0:
                    act.wait_ge(neg_ready, b + 1)
                if s == NSEG - 1:
                    nc.scalar.activation(mask_c[0:SP, u, :], mask_n[0:SP, :], ACT.Copy, scale=-MASKED, bias=MASKED)
                at = slice(s * SEG, (s + 1) * SEG)
                nc.scalar.activation(mask_b[:, at], mask_u8[:, at], ACT.Copy, scale=-MASKED, bias=MASKED
                                     ).then_inc(mask_ready, 1)

            def out_turn(b, j, turn, a):
                lo, hi = (0, 512) if j == 0 else (512, Q)
                act.wait_ge(a_full, turn)
                nc.scalar.activation(q_all[:, bass.ds(b[1], 1), 0, lo:hi].rearrange("p b q -> p (b q)"),
                                     a_ps[:, a, 0:hi - lo], ACT.Copy).then_inc(ot_hi, 1)

            def exponentials(b, k, first, between=lambda: None):
                n = b * NC + k
                act.wait_ge(shifted, n + 1)
                if not (first and k < NPB):
                    act.wait_ge(summed, n - NPB + 1)
                scores = sc_ps[k % 2][0:SP, :, 0:HALF]
                nc.scalar.activation(p_hl[0:SP, k % NPB, 0, :].rearrange("p (a n) -> p a n", a=2), scores,
                                     ACT.Exp).then_inc(p_hi_ready, 1)
                between()
                if not (first and k < 2):
                    act.wait_ge(p_ready, n - 1)
                nc.scalar.activation(p_f[0:SP, k % 2, :].rearrange("p (a n) -> p a n", a=2), scores,
                                     ACT.Exp).then_inc(p_f_ready, 1)

            def normalise(b):
                act.wait_ge(dve_o, b * 2 + 2)
                for t in range(3):
                    nc.scalar.activation(o_f[:, t, :], o_ps[:, 0, t * VC:t * VC + DV], ACT.Copy,
                                             scale=rden[:, t:t + 1])
                s = nc.scalar.activation(o_f[:, 6, 0:CUT], o_ps[:, 0, 3 * VC:], ACT.Copy, scale=rden[:, 6:7])
                s.then_inc(o_act, 1)

            def batch(g, i, u, v, first, last):
                b = g * GB + i
                plan = turn_plan(not last, not first)
                turn, base = [0], turns_before(g, i)

                def fill(k, slots):
                    for kind, j in sum([plan[k][slot] for slot in slots], []):
                        turn[0] += 1
                        if kind == "out":
                            out_turn((b, i - 1), j, base + turn[0], (turn[0] - 1) % 2)

                def next_keys(k, step):
                    kind, s = KEY_STEPS.get((k, step), ("", 0)) if not last else ("", 0)
                    if first and (kind, s) in EARLY:
                        pass
                    elif kind == "ct":
                        split_ct(b + 1, 1 - u, first, s)
                    elif kind == "mask":
                        masks(b + 1, 1 - u, s)
                    elif kind == "c":
                        split_c(b + 1, 1 - u, first)

                for k in range(NC):
                    if first and k == 3:
                        act.wait_ge(stored, g * 16 + 16)
                        act.dma_start(xg[0:TT, :, :], x[bass.ds(g * GT, GT), :].rearrange("(t p) n -> p t n", p=TT)
                                      ).then_inc(x_in, 16)
                    if k == LAG - 1 and not first:
                        normalise(b - 1)
                    fill(k, (0, 1))
                    next_keys(k, 0)
                    if not (first and k == 0):
                        exponentials(b, k, first, lambda: next_keys(k, 1))
                    fill(k, (2, 3))
                    next_keys(k, 2)

            def load_next(g):
                act.dma_start(x_next[0:TT, :, :], x[bass.ds(g * GT, GT), :].rearrange("(t p) n -> p t n", p=TT)
                              ).then_inc(x_next_in, 16)

            def queries(g, heads=range(H)):
                for h in heads:
                    act.wait_ge(q_full, g * H + h + 1)
                    nc.scalar.activation(q_all[:, :, 0, h * T:(h + 1) * T],
                                         banks[h % 4][:, 0:GT].rearrange("p (b t) -> p b t", b=GB), ACT.Copy,
                                         scale=1 / WS).then_inc(q_hi_ready, 1)

            def first_keys(b0):
                for s in range(NSEG):
                    split_ct(b0, 0, True, s)
                    masks(b0, 0, s)
                split_c(b0, 0, True)

            def early_keys(b):
                for kind, s in EARLY:
                    if kind == "ct":
                        split_ct(b, 1, True, s)
                    else:
                        masks(b, 1, s)

            run = body_loop(act, batch)

            def group(g, has_next):
                run(g)
                b_last, ln_next, ln_own = g * GB + GB - 1, *ln_of(g, has_next)
                normalise(b_last)
                for j in range(N_O):
                    out_turn((b_last, GB - 1), j, (g + 1) * ((N_M + N_O) * GB) - N_O + j + 1, j)
                if has_next:
                    load_next(g + 1)
                    root(ln_next)
                    first_keys(g * GB + GB)
                for k in range(KD):
                    act.wait_ge(proj_full, g * KD + k + 1)
                    nc.scalar.activation(proj_t[:, k, :], banks[k][:, 0:GT], ACT.Copy).then_inc(proj_copied, 1)
                    if k == 0 and has_next:
                        split_x(ln_next, False, xt_next_hl)
                if has_next:
                    queries(g + 1, range(0, ROOT_AT))
                root(ln_own)
                if has_next:
                    queries(g + 1, range(ROOT_AT, TURN_X_AT))
                split_x(ln_own, True)
                if has_next:
                    queries(g + 1, range(TURN_X_AT, ROUTER_AT))
                act.wait_ge(logits_full, g + 1)
                nc.scalar.activation(r_exp[0:TT, :, :].rearrange("p t e -> p (t e)"), a_ps[0:TT, 0, 0:NT * E], ACT.Exp,
                                     scale=-1.0).then_inc(r_exp_ready, 1)
                if has_next:
                    queries(g + 1, range(ROUTER_AT, H))
                for j in range(NH):
                    act.wait_ge(h_full, g * NH + j + 1)
                    if j >= 2:
                        act.wait_ge(h_step, (g * NH + j - 2) * 3 + 1)
                    nc.scalar.activation(s_f[:, j % 2, :], sc_ps[j % 2][:, 0, 0:GT], ACT.Silu, scale=1 / WS
                                         ).then_inc(silu_ready, 1)
                if has_next:
                    early_keys(g * GB + GB + 1)
                    act.wait_ge(h_used, g * NH + NH - 1)
                    exponentials(g * GB + GB, 0, True)
                act.wait_ge(y_ready, g * NT + NT + 1)
                act.dma_start(out[bass.ds(g * GT, GT), :].rearrange("(t p) n -> p t n", p=TT), xg[0:TT, :, :]
                              ).then_inc(stored, 16)

            load_next(0)
            root(0)
            for n in range(N_MIX):
                (hi, _), scale = mix_out(n)
                act.wait_ge(mix_made, n + 1)
                nc.scalar.activation(hi, mix_ps(n), ACT.Copy, scale=scale).then_inc(mix_hi, 1)
            act.wait_ge(consts_in, 16 * N_CONSTS)
            nc.scalar.activation(gates_th[:, :], gates_in[:, :], ACT.Tanh).then_inc(th_ready, 1)
            split_x(0, False)
            queries(0, range(0, W1_AT))
            act.wait_ge(w1_in, 16)
            nc.scalar.activation(w1_hl[0][:, :, 0:HID], w1_f, ACT.Copy, scale=WS).then_inc(w1_hi, 1)
            queries(0, range(W1_AT, W3_AT[0]))
            act.wait_ge(w3_in, 16)
            nc.scalar.activation(w3_f, w3_f, ACT.Copy, scale=WS).then_inc(w3_scaled, 1)
            queries(0, range(W3_AT[0], W3_AT[1]))
            act.wait_ge(w3_scaled, 1)
            nc.scalar.activation(w3_hl[0][:, :, 0:HID], w3_f, ACT.Copy).then_inc(w3_hi, 1)
            queries(0, range(W3_AT[1], H))
            first_keys(0)
            act.wait_ge(w1_ready, 1)
            act.wait_ge(w2_in, 48)
            act.wait_ge(zeroed_w2, 1)
            for w_f, _ in w2_parts:
                nc.scalar.activation(w_f, w_f, ACT.Copy, scale=WS).then_inc(w2_scaled, 1)
            for n, (w_f, tiles) in enumerate(w2_parts):
                act.wait_ge(w2_scaled, n + 1)
                nc.scalar.activation(w2_hl[0][:, tiles, :], w_f, ACT.Copy).then_inc(w2_hi, 1)
            act.wait_ge(w3_ready, 1)
            act.wait_ge(w2_ready, 2)
            early_keys(1)
            exponentials(0, 0, True)
            all_groups(act, group)
            act.wait_ge(stored, (G + 1) * 16)

        @block.vector
        def _(dve):
            dve.sem_inc(neg_ready, 1)
            dve.sem_inc(y_ready, 1)
            nc.vector.memset(shift_m[:, :], 0.0).then_inc(zeroed_dve, 1)
            nc.vector.memset(neg_pad[:, :], 0.0).then_inc(zeroed_dve, 1)
            nc.vector.memset(w2_f[1][HLAST:128, NH - 1 - NHA, :], 0.0).then_inc(zeroed_w2, 1)
            nc.vector.memset(nothing[:, 4:5], 0.0)
            nc.vector.memset(g_pad[:, :, :], 0.0).then_inc(zeroed_dve, 1)
            dve.wait_ge(zeroed_dve, 3)
            nc.vector.memset(g_pad[:, :, E:E + 1], 1.0).then_inc(zeroed_dve, 1)
            dve.wait_ge(zeroed_dve, 4)

            def carry_wait(column):
                nc.vector.tensor_copy(nothing[:, column:column + 1], nothing[:, 4:5])

            def layer_norm(n, src, meanwhile=lambda: None):
                for t in range(NT):
                    s = nc.vector.bn_stats(stats[0:TT, t, :], src[0:TT, t, :])
                s.then_inc(ln_step, 1)
                dve.wait_ge(ln_step, n * 3 + 1)
                carry_wait(3)
                for t in range(NT):
                    s = nc.vector.bn_aggr(mv[0:TT, t, :], stats[0:TT, t, :])
                s.then_inc(ln_step, 1)
                dve.wait_ge(ln_step, n * 3 + 2)
                nc.vector.tensor_scalar(var_eps[0:TT, :], mv[0:TT, :, 1], EPS, None, ALU.add).then_inc(ln_step, 1)
                meanwhile()
                dve.wait_ge(ln_sd, n + 1)
                nc.vector.reciprocal(rstd[0:TT, :], sd[0:TT, :]).then_inc(ln_rstd, 1)
                dve.wait_ge(ln_rstd, n + 1)
                for t in range(NT):
                    nc.vector.tensor_scalar(xn[0:TT, t, :], src[0:TT, t, :], mv[0:TT, t, 0:1], rstd[0:TT, t:t + 1],
                                            ALU.subtract, ALU.mult).then_inc(xn_ready, 1)

            def split_x(n, to=xt_hl):
                for k in range(KD):
                    dve.wait_ge(xt_hi_ready, n * KD + k + 1)
                    nc.vector.tensor_tensor(to[1][:, k, :], o_ps[:, k, 0:GT], to[0][:, k, :], ALU.subtract
                                            ).then_inc(xt_ready, 1)

            def queries(g, heads=range(H)):
                for h in heads:
                    dve.wait_ge(q_hi_ready, g * H + h + 1)
                    at = slice(h * T, (h + 1) * T)
                    nc.vector.scalar_tensor_tensor(q_all[:, :, 1, at],
                                                   banks[h % 4][:, 0:GT].rearrange("p (b t) -> p b t", b=GB), 1 / WS,
                                                   q_all[:, :, 0, at], ALU.mult, ALU.subtract).then_inc(q_ready, 1)

            def seg(b, n, turn, bank, a):
                s, j = n // NQ, n % NQ
                if j == 0:
                    dve.wait_ge(mask_ready, b * NSEG + s + 1)
                    carry_wait(2)
                dve.wait_ge(a_full, turn)
                carry_wait(a)
                nc.vector.tensor_tensor_reduce(max_junk[a], bank[:, 0:SEG], mask_b[:, s * SEG:(s + 1) * SEG],
                                               1.0, -3e38, ALU.add, ALU.max, maxes[:, j, s:s + 1]
                                               ).then_inc(a_used, 1)
                return j, s

            def negate(b, turn):
                dve.wait_ge(a_used, turn)
                nc.vector.tensor_reduce(neg_max[:, :], maxes[:, :, :], AX.X, ALU.max, negate=True).then_inc(dve_m, 1)
                dve.wait_ge(dve_m, m_of(b) + 1)
                for at in (0, LOW):
                    s = nc.vector.tensor_scalar(neg_pad[:, at:at + NQ], neg_max[:, :], 1e28, None, ALU.min)
                s.then_inc(neg_ready, 1)

            def row(b, u, j, turn, bank):
                lo, hi = (0, 512) if j == 0 else (512, Q)
                dve.wait_ge(a_full, turn)
                nc.vector.tensor_copy(shift_b[:, u, lo:hi], bank[:, 0:hi - lo]).then_inc(a_used, 1)

            def shift(b, turn, bank):
                dve.wait_ge(a_full, turn)
                nc.vector.tensor_copy(max_hi[:, :], bank[0:64, 0:128]).then_inc(dve_m, 1)
                dve.wait_ge(dve_m, m_of(b) + 2)
                nc.vector.scalar_tensor_tensor(shift_m[0:64, :], max_hi[:, :], low_rows[:, 0:1], bank[0:64, 0:128],
                                               ALU.mult, ALU.add).then_inc(a_used, 1)

            def normalise(b):
                dve.wait_ge(summed, b * NC + NC)
                six = o_ps[:, 0:2, 0:3 * VC].rearrange("p a (j n) -> p a j n", j=3)
                seventh = o_ps[:, 1, 3 * VC:3 * VC + VC - CUT]
                nc.vector.tensor_scalar(den[:, 0:6].rearrange("p (a j) -> p a j", a=2), six[:, :, :, DV], 1e-30, None,
                                        ALU.max)
                nc.vector.tensor_scalar(den[:, 6:7], seventh[:, DV - CUT:VC - CUT], 1e-30, None, ALU.max).then_inc(dve_o, 1)
                dve.wait_ge(dve_o, b * 2 + 1)
                nc.vector.reciprocal(rden[:, :], den[:, :]).then_inc(dve_o, 1)
                dve.wait_ge(dve_o, b * 2 + 2)
                nc.vector.tensor_tensor(o_f[:, 3:6, :], six[:, 1, :, 0:DV],
                                        rden[:, 3:6].unsqueeze(2).broadcast_to([128, 3, DV]), ALU.mult)
                nc.vector.tensor_scalar(o_f[:, 6, CUT:DV], seventh[:, 0:DV - CUT], rden[:, 6:7], None, ALU.mult
                                        ).then_inc(o_ready, 1)

            def out_turn(b, i, j, a):
                lo, hi = (0, 512) if j == 0 else (512, Q)
                dve.wait_ge(ot_hi, b * N_O + j + 1)
                nc.vector.tensor_tensor(q_all[:, bass.ds(i, 1), 1, lo:hi].rearrange("p b q -> p (b q)"),
                                        a_ps[:, a, 0:hi - lo],
                                        q_all[:, bass.ds(i, 1), 0, lo:hi].rearrange("p b q -> p (b q)"),
                                        ALU.subtract).then_inc(a_used, 1)

            def add_shift(b, k, u, turns):
                dve.wait_ge(scored, b * NC + k + 2)
                if k == 0:
                    dve.wait_ge(a_used, turns)
                halves = sc_ps[k % 2][0:SP, :, 0:HALF]
                nc.vector.scalar_tensor_tensor(halves, halves, mask_c[0:SP, u, k:k + 1],
                                               shift_b[0:SP, u, :].rearrange("p (a n) -> p a n", a=2),
                                               ALU.add, ALU.add).then_inc(shifted, 1)

            def take(kind, j, g, i, u, base, n, places):
                b, turn, a, bank = g * GB + i, base + n, (n - 1) % 2, places[(n - 1) % len(places)]
                if kind == "seg":
                    seg(b + 1, j, turn, bank, a)
                    if j == N_SEG - 1:
                        negate(b + 1, turn)
                elif kind == "max":
                    shift(b + 1, turn, bank)
                elif kind == "row":
                    row(b + 1, 1 - u, j, turn, bank)
                elif kind == "out":
                    out_turn(b - 1, i - 1, j, a)

            def batch(g, i, u, v, first, last):
                b = g * GB + i
                plan = turn_plan(not last, not first)
                turn, base = 0, turns_before(g, i)
                for k in range(NC):
                    for slot in range(4):
                        if slot == 1:
                            if k == LAG - 1 and not first:
                                normalise(b - 1)
                            if not (first and k == 0):
                                add_shift(b, k, u, base)
                        for kind, j in plan[k][slot]:
                            turn += 1
                            take(kind, j, g, i, u, base, turn, a_banks)

            run = body_loop(dve, batch)

            def group(g, has_next):
                run(g)
                b_last, ln_next, ln_own = g * GB + GB - 1, *ln_of(g, has_next)
                normalise(b_last)
                for j in range(N_O):
                    out_turn(b_last, GB - 1, j, j)
                if has_next:
                    dve.wait_ge(x_next_in, g * 16 + 32)
                    layer_norm(ln_next, x_next)
                    split_x(ln_next, xt_next_hl)
                dve.wait_ge(x_in, g * 16 + 16)
                dve.wait_ge(proj_back, g * KD + KD)
                for t in range(NT):
                    nc.vector.scalar_tensor_tensor(xg[0:TT, t, :], banks[2 + t // 2][0:TT, (t % 2) * D:(t % 2 + 1) * D],
                                                   gates[0:TT, 0:1],
                                                   xg[0:TT, t, :], ALU.mult, ALU.add).then_inc(x2_ready, 1)
                dve.wait_ge(x2_ready, g * NT + NT)
                if has_next:
                    layer_norm(ln_own, xg, lambda: queries(g + 1, range(0, ROOT_AT)))
                    queries(g + 1, range(ROOT_AT, TURN_X_AT))
                    split_x(ln_own)
                    queries(g + 1, range(TURN_X_AT, ROUTER_AT))
                else:
                    layer_norm(ln_own, xg)
                    split_x(ln_own)

                r0 = g * 11

                def step(ins, n):
                    ins.then_inc(r_step, 1)
                    dve.wait_ge(r_step, r0 + n)
                flat = "p t e -> p (t e)"
                dve.wait_ge(r_exp_ready, g + 1)
                step(nc.vector.tensor_scalar(r_one[0:TT, :, :], r_exp[0:TT, :, :], 1.0, None, ALU.add), 1)
                step(nc.vector.reciprocal(score[0:TT, :, :], r_one[0:TT, :, :]), 2)
                step(nc.vector.tensor_tensor(sel[0:TT, :, :], score[0:TT, :, :],
                                             bias_sb[0:TT, :].unsqueeze(1).broadcast_to([TT, NT, E]), ALU.add), 3)
                for t in range(NT):
                    other = sel[0:TT, t, :].unsqueeze(1).broadcast_to([TT, E, E])
                    own = sel[0:TT, t, :].unsqueeze(2).broadcast_to([TT, E, E])
                    nc.vector.tensor_tensor(ahead[0:TT, t, :, :], other, own, ALU.is_gt)
                    s = nc.vector.tensor_tensor(tied[0:TT, t, :, :], other, own, ALU.is_equal)
                step(s, 4)
                step(nc.vector.tensor_tensor(tied[0:TT, :, :, :].rearrange("p t e f -> p t (e f)"),
                                             tied[0:TT, :, :, :].rearrange("p t e f -> p t (e f)"),
                                             before_sb[0:TT, :].unsqueeze(1).broadcast_to([TT, NT, E * E]),
                                             ALU.mult), 5)
                step(nc.vector.tensor_tensor(ahead[0:TT, :, :, :], ahead[0:TT, :, :, :], tied[0:TT, :, :, :],
                                             ALU.add), 6)
                if has_next:
                    queries(g + 1, range(ROUTER_AT, H))
                step(nc.vector.tensor_reduce(rank[0:TT, :, :], ahead[0:TT, :, :, :], AX.X, ALU.add), 7)
                step(nc.vector.scalar_tensor_tensor(w_top[0:TT, :, :], rank[0:TT, :, :], TOPK - 0.5,
                                                    score[0:TT, :, :], ALU.is_lt, ALU.mult), 8)
                step(nc.vector.tensor_reduce(w_sum[0:TT, :], w_top[0:TT, :, :], AX.X, ALU.add), 9)
                step(nc.vector.tensor_scalar(w_sum[0:TT, :], w_sum[0:TT, :], 1e-12, None, ALU.max), 10)
                step(nc.vector.reciprocal(w_rec[0:TT, :], w_sum[0:TT, :]), 11)
                for at in (0, LOW):
                    s = nc.vector.tensor_tensor(g_pad[0:TT, :, at:at + E], w_top[0:TT, :, :],
                                                w_rec[0:TT, :].unsqueeze(2).broadcast_to([TT, NT, E]), ALU.mult)
                s.then_inc(gate_ready, 1)
                dve.wait_ge(g_full, g + 1)
                nc.vector.tensor_copy(g_hi[:, :], a_ps[0:64, 0, 0:GT]).then_inc(g_ready, 1)
                dve.wait_ge(g_ready, g * 2 + 1)
                nc.vector.scalar_tensor_tensor(g_t[0:64, :], g_hi[:, :], low_rows[:, 0:1], a_ps[0:64, 0, 0:GT],
                                               ALU.mult, ALU.add).then_inc(g_ready, 1)
                next_turn0, taken = (g + 1) * ((N_M + N_O) * GB), [0]

                def turns(number):
                    for kind, j in FIRST[taken[0]:taken[0] + number] if has_next else ():
                        taken[0] += 1
                        take(kind, j, g + 1, -1, 1, next_turn0, taken[0], ffn_bank)

                for j in range(NH):
                    n = g * NH + j
                    turns(TURNS_AROUND[j][0])
                    dve.wait_ge(silu_ready, n + 1)
                    if j >= 2:
                        dve.wait_ge(h_used, n - 1)
                    nc.vector.tensor_tensor(v_f[:, 0, :], sc_ps[j % 2][:, 1, 0:GT], s_f[:, j % 2, :], ALU.mult
                                            ).then_inc(h_step, 1)
                    dve.wait_ge(h_step, n * 3 + 1)
                    dve.wait_ge(e_full, n + 1)
                    nc.vector.scalar_tensor_tensor(v_f[:, 1, :], v_f[:, 0, :], 1 / WS, o_ps[:, 0, 0:GT],
                                                   ALU.mult, ALU.mult).then_inc(h_step, 1)
                    dve.wait_ge(h_step, n * 3 + 2)
                    nc.vector.tensor_copy(h_hl[:, j % 2, 0, 0:GT], v_f[:, 1, :]).then_inc(h_step, 1)
                    dve.wait_ge(h_step, n * 3 + 3)
                    nc.vector.tensor_tensor(h_hl[:, j % 2, 1, 0:GT], v_f[:, 1, :], h_hl[:, j % 2, 0, 0:GT],
                                            ALU.subtract).then_inc(h_ready, 1)
                    turns(TURNS_AROUND[j][1])
                if has_next:
                    add_shift(g * GB + GB, 0, 0, next_turn0 + N_M)
                dve.wait_ge(h_used, g * NH + NH)
                for t in range(NT):
                    acc = a_ps[0:TT, t // 2, (t % 2) * D:(t % 2 + 1) * D]
                    nc.vector.scalar_tensor_tensor(xg[0:TT, t, :], acc, gates[0:TT, 1:2], xg[0:TT, t, :],
                                                   ALU.mult, ALU.add).then_inc(y_ready, 1)

            dve.wait_ge(x_next_in, 16)
            layer_norm(0, x_next)
            for n in range(N_MIX):
                (hi, lo), scale = mix_out(n)
                dve.wait_ge(mix_hi, n + 1)
                nc.vector.scalar_tensor_tensor(lo, mix_ps(n), scale, hi, ALU.mult, ALU.subtract
                                               ).then_inc(mix_used, 1)
            split_x(0)
            dve.wait_ge(th_ready, 1)
            nc.vector.tensor_scalar(gates[:, 0:1], gates_th[:, 0:1], 1 / NS, None, ALU.mult).then_inc(gates_ready, 1)
            nc.vector.tensor_scalar(gates[:, 1:2], gates_th[:, 1:2], 1 / WS, None, ALU.mult).then_inc(gates_ready, 1)
            queries(0, range(0, W1_AT))
            dve.wait_ge(w1_hi, 1)
            nc.vector.scalar_tensor_tensor(w1_hl[1][:, :, 0:HID], w1_f, WS, w1_hl[0][:, :, 0:HID], ALU.mult, ALU.subtract
                                           ).then_inc(w1_ready, 1)
            queries(0, range(W1_AT, H))
            dve.wait_ge(gates_ready, 2)
            dve.wait_ge(consts_in, 16 * N_CONSTS)
            dve.wait_ge(late_consts_in, 64)
            for n, (kind, j) in enumerate(FIRST):
                take(kind, j, 0, -1, 1, 0, n + 1, a_banks)
            add_shift(0, 0, 0, N_M)
            all_groups(dve, group)

        @block.tensor
        def _(pe):
            def product(outs, lhs, rhs, first=True, last=True, **kw):
                mm = None
                for n, (a, c) in enumerate(((0, 0), (0, 1), (1, 0))):
                    mm = nc.tensor.matmul(outs, lhs[a], rhs[c], start=first and n == 0, stop=last and n == 2, **kw)
                return mm

            pe.sem_inc(scored, 1)
            pe.wait_ge(wk_in, 16)
            for n in range(N_MIX):
                h = n % H
                if n == H:
                    pe.wait_ge(wv_in, 16)
                if h % (H // 2) == 0:
                    pe.wait_ge((wq_in if n < H else wo_in)[h // (H // 2)], 16)
                if n >= 4:
                    pe.wait_ge(mix_used, n - 3)
                if n < H:
                    for k in range(KD):
                        mm = nc.tensor.matmul(mix_ps(n)[:, k, :], wq_f[:, h, k * 128:(k + 1) * 128],
                                              wk_f[:, h // 2, :], start=True, stop=True)
                else:
                    mm = nc.tensor.matmul(mix_ps(n), wv_f[:, h // 2, :], wo_f[:, h, :], start=True, stop=True)
                mm.then_inc(mix_made, 1)
            pe.wait_ge(id_in, 16)

            def transpose_x(n):
                pe.wait_ge(xn_ready, n * NT + NT)
                for k in range(KD):
                    for t in range(NT):
                        mm = nc.tensor.transpose(o_ps[:, k, t * TT:(t + 1) * TT], xn[0:TT, t, k * 128:(k + 1) * 128],
                                                 id_sb[0:TT, 0:TT])
                    mm.then_inc(xt_full, 1)

            def queries(g, heads=range(H), tokens=xt_next_hl):
                for h in heads:
                    if h >= 4:
                        pe.wait_ge(q_ready, g * H + h - 3)
                    for k in range(KD):
                        mm = product(banks[h % 4][:, 0:GT], [m[:, k, h, :] for m in m_hl],
                                     [xt[:, k, :] for xt in tokens], k == 0, k == KD - 1)
                    mm.then_inc(q_full, 1)

            def take(kind, j, g, i, u, v, base, n, places=a_banks, start=False):
                b, bank = g * GB + i, places[(n - 1) % len(places)]
                if kind == "row" and j == 0:
                    pe.wait_ge(a_used, base + (n - 1))
                elif not start or n > len(places):
                    pe.wait_ge(a_used, base + (n - len(places)))
                if kind == "seg":
                    s, t = j // NQ, j % NQ
                    if t == 0:
                        pe.wait_ge(ct_hi_ready, (b + 1) * NSEG + s + 1)
                    if j == 0:
                        pe.wait_ge(staged[1 - u], (v + u + 1) * 16)
                    mm = nc.tensor.matmul(bank[:, 0:SEG], q_st[:, 1 - u, 0, t * 128:(t + 1) * 128],
                                          ct[1 - u][0][:, s * SEG:(s + 1) * SEG], start=True, stop=True)
                elif kind == "row":
                    for t in (range(0, 4) if j == 0 else range(4, NQ)):
                        mm = nc.tensor.matmul(bank[:, (t % 4) * 128:(t % 4 + 1) * 128], pick_sb[:, t, :],
                                              shift_m[:, :], start=True, stop=True)
                elif kind == "max":
                    pe.wait_ge(neg_ready, b + 3)
                    mm = nc.tensor.transpose(bank[:, 0:128], neg_pad[:, :], id_sb[:, :])
                else:
                    if j == 0:
                        pe.wait_ge(o_ready, b)
                        pe.wait_ge(o_act, b)
                    for t in (range(0, 4) if j == 0 else range(4, NQ)):
                        mm = nc.tensor.transpose(bank[:, (t % 4) * 128:(t % 4 + 1) * 128], o_f[:, t, :], id_sb[:, :])
                mm.then_inc(a_full, 1)

            def scores(b, k, u, v, first, slot0):
                n = b * NC + k
                if not (first and k < 2):
                    pe.wait_ge(p_f_ready, n - 1)
                if k == 0:
                    pe.wait_ge(split_done, b * 2 + 2)
                keys_k = slice(k * SP, (k + 1) * SP)
                for n_pass, (kp, qp) in enumerate(((0, 0), (0, 1), (1, 0))):
                    for a in range(2):
                        mm = nc.tensor.matmul(sc_ps[k % 2][0:SP, a, 0:HALF], ct[u][kp][:, keys_k],
                                              q_st[:, u, qp, a * HALF:(a + 1) * HALF], start=n_pass == 0, stop=n_pass == 2)
                    if n_pass == 0:
                        slot0()
                mm.then_inc(scored, 1)

            def weighted(b, k, u, first, slot2):
                pe.wait_ge(p_ready, b * NC + k + 1)
                if k == 0:
                    pe.wait_ge(split_done, b * 2 + 3)
                    if not first:
                        pe.wait_ge(o_ready, b)
                        pe.wait_ge(o_act, b)
                hi, lo = p_hl[0:SP, k % NPB, 0, :], p_hl[0:SP, k % NPB, 1, :]
                for t in range(NQ):
                    q = slice(t * 128, (t + 1) * 128)
                    pieces = [(t // 3, (t % 3) * VC, 0, VC)] if t < 6 else [(0, 3 * VC, 0, CUT), (1, 3 * VC, CUT, VC)]
                    for n, (p, c, w) in enumerate(((hi, 0, VC), (hi, VC, DV), (lo, 0, VC))):
                        for bank, at, c0, c1 in pieces:
                            c1 = min(c1, w)
                            mm = nc.tensor.matmul(o_ps[:, bank, at:at + c1 - c0], p[:, q],
                                                  cv[u][0:SP, k, c + c0:c + c1],
                                                  start=k == 0 and t in (0, 3) and n == 0,
                                                  stop=k == NC - 1 and n == 2, skip_group_check=True)
                    if t == 3:
                        slot2()
                mm.then_inc(summed, 1)

            def batch(g, i, u, v, first, last):
                b = g * GB + i
                plan = turn_plan(not last, not first)
                base = turns_before(g, i)
                before = [0]

                def fill(k, slot):
                    for kind, j in plan[k][slot]:
                        before[0] += 1
                        take(kind, j, g, i, u, v, base, before[0])

                for k in range(NC):
                    if k == LAG - 1 and not first:
                        weighted(b - 1, NC - 1, 1 - u, False, lambda: None)
                    if not (first and k == 0):
                        scores(b, k, u, v, first, lambda: fill(k, 0))
                    if first and k == 1:
                        pe.wait_ge(y_ready, g * NT + 1)
                    fill(k, 1)
                    if k >= LAG:
                        weighted(b, k - LAG, u, first, lambda: fill(k, 2))
                    elif k < LAG - 1 and not first:
                        weighted(b - 1, NC - LAG + k, 1 - u, False, lambda: fill(k, 2))
                    else:
                        fill(k, 2)
                    fill(k, 3)

            run = body_loop(pe, batch)

            def group(g, has_next):
                run(g)
                b_last, ln_next, ln_own = g * GB + GB - 1, *ln_of(g, has_next)
                next_turn0 = (g + 1) * ((N_M + N_O) * GB)
                for k in range(NC - LAG, NC):
                    weighted(b_last, k, 1, False, lambda: None)
                for j in range(N_O):
                    take("out", j, g, GB, 0, 0, next_turn0 - N_O, j + 1)
                pe.wait_ge(a_used, next_turn0)
                for k in range(KD):
                    for h in range(H):
                        ot = [q_all[:, :, p, h * T:(h + 1) * T] for p in range(2)]
                        mm = product(banks[k][:, 0:GT], [n_[:, h, k * 128:(k + 1) * 128] for n_ in n_hl], ot,
                                     h == 0, h == H - 1)
                    mm.then_inc(proj_full, 1)
                    if k == 0 and has_next:
                        transpose_x(ln_next)
                for k in range(KD):
                    pe.wait_ge(proj_copied, g * KD + k + 1)
                    for t in range(NT):
                        mm = nc.tensor.transpose(banks[2 + t // 2][0:TT, (t % 2) * D + k * 128:(t % 2) * D + (k + 1) * 128],
                                                 proj_t[:, k, t * TT:(t + 1) * TT], id_sb[:, :])
                    mm.then_inc(proj_back, 1)
                if has_next:
                    pe.wait_ge(xt_ready, ln_next * KD + KD)
                    queries(g + 1, range(0, 2))
                pe.wait_ge(x2_ready, g * NT + NT)
                if has_next:
                    queries(g + 1, range(2, TURN_X_AT))
                transpose_x(ln_own)
                if has_next:
                    queries(g + 1, range(TURN_X_AT, LOGITS_AT))
                pe.wait_ge(xt_ready, ln_own * KD + KD)
                for t in range(NT):
                    for k in range(KD):
                        mm = nc.tensor.matmul(a_ps[0:TT, 0, t * E:(t + 1) * E], xt_f[:, k, t * TT:(t + 1) * TT],
                                              gate_sb[:, k, :], start=k == 0, stop=k == KD - 1)
                mm.then_inc(logits_full, 1)
                if has_next:
                    queries(g + 1, range(LOGITS_AT, H))
                    pe.wait_ge(q_ready, (g + 1) * H + H - 2)

                def hidden(j):
                    hid = slice(j * 128, (j + 1) * 128)
                    for a, w in enumerate((w1_hl, w3_hl)):
                        for k in range(KD):
                            mm = product(sc_ps[j % 2][:, a, 0:GT], [p[:, k, hid] for p in w],
                                         [xt[:, k, :] for xt in xt_hl], k == 0, k == KD - 1)
                    mm.then_inc(h_full, 1)

                def down(j):
                    pe.wait_ge(h_ready, g * NH + j + 1)
                    for t in range(NT):
                        acc = a_ps[0:TT, t // 2, (t % 2) * D:(t % 2 + 1) * D]
                        hid = [h_hl[:, j % 2, p, t * TT:(t + 1) * TT] for p in range(2)]
                        mm = product(acc, hid, [w[:, j, :] for w in w2_hl], j == 0 and t % 2 == 0, j == NH - 1,
                                     skip_group_check=True)
                    mm.then_inc(h_used, 1)

                taken = [0]

                def turns(number):
                    for kind, j in FIRST[taken[0]:taken[0] + number] if has_next else ():
                        taken[0] += 1
                        take(kind, j, g + 1, -1, 1, (g + 1) * (GB // 2) - 1, next_turn0, taken[0], ffn_bank, start=True)

                hidden(0)
                if has_next:
                    pe.wait_ge(q_ready, (g + 1) * H + H)
                hidden(1)
                pe.wait_ge(gate_ready, g + 1)
                for t in range(NT):
                    mm = nc.tensor.transpose(a_ps[:, 0, t * TT:(t + 1) * TT], g_pad[0:TT, t, :], id_sb[0:TT, 0:TT])
                mm.then_inc(g_full, 1)
                for j in range(NH):
                    if j >= 2:
                        pe.wait_ge(h_ready, g * NH + j - 1)
                        hidden(j)
                    turns(TURNS_AROUND[j][0])
                    if j == 0:
                        pe.wait_ge(g_ready, g * 2 + 2)
                    else:
                        pe.wait_ge(h_step, (g * NH + j - 1) * 3 + 2)
                    nc.tensor.matmul(o_ps[:, 0, 0:GT], expand_sb[:, j * 128:(j + 1) * 128], g_t[:, :],
                                     start=True, stop=True).then_inc(e_full, 1)
                    if j >= 1:
                        down(j - 1)
                    turns(TURNS_AROUND[j][1])
                if has_next:
                    scores(g * GB + GB, 0, 0, 0, True, lambda: None)
                down(NH - 1)
                if has_next:
                    pe.wait_ge(a_used, next_turn0 + N_M)

            transpose_x(0)
            pe.wait_ge(xt_ready, KD)
            queries(0, tokens=xt_hl)
            pe.wait_ge(consts_in, 16 * N_CONSTS)
            for n, (kind, j) in enumerate(FIRST):
                take(kind, j, 0, -1, 1, -1, 0, n + 1, start=True)
            pe.wait_ge(q_ready, H)
            pe.wait_ge(w1_ready, 1)
            pe.wait_ge(w3_ready, 1)
            pe.wait_ge(w2_ready, 2)
            pe.wait_ge(zeroed, N_ZERO)
            pe.wait_ge(late_consts_in, 64)
            scores(0, 0, 0, 0, True, lambda: None)
            all_groups(pe, group)


def kernel(x, ctx_1024, mask_BxS2_bf1, g_xattn, g_ffn, L0_xattn_Wq, L0_xattn_Wk, L0_xattn_Wv, L0_xattn_Wo,
           L0_ffn_gate_w, L0_ffn_router_bias, L0_ffn_W1, L0_ffn_W3, L0_ffn_W2, L0_ffn_sw1, L0_ffn_sw3, L0_ffn_sw2):
    import numpy as np
    import concourse.bacc as bacc
    from concourse import mybir as mb
    from concourse.bass_utils import run_bass_kernel_spmd as launch

    def lay(a):
        return np.ascontiguousarray(a)

    ctx_h = np.asarray(ctx_1024)
    mask_h = np.asarray(mask_BxS2_bf1).view(np.uint8)
    pick = np.zeros((128, NQ, 128), mb.dt.np(BF16))
    for j in range(NQ):
        pick[j, j], pick[LOW + j, j] = 1, 1
    expand = np.zeros((128, NH * 128), np.float16)
    for j in range(HID):
        e = min(j // INTER, E)
        expand[e, j] = 1
        if e < E:
            expand[LOW + e, j] = 1
    before = np.zeros((128, E * E), np.float32)
    for e in range(E):
        before[:, e * E:e * E + e] = 1
    low = np.zeros((64, 1), np.float32)
    low[LOW:] = -1
    w1, w3, w2 = np.asarray(L0_ffn_W1), np.asarray(L0_ffn_W3), np.asarray(L0_ffn_W2)
    arrays = {
        "x": lay(np.asarray(x).reshape(B * T, D)),
        "ctx": lay(ctx_h),
        "ctxT": lay(ctx_h.reshape(B, SP, NC, DV).transpose(0, 3, 2, 1).reshape(B, DV, S)),
        "mask": lay(mask_h),
        "maskT": lay(mask_h.reshape(B, SP, NC).transpose(0, 2, 1).reshape(B, S)),
        "g_xattn": lay(g_xattn), "g_ffn": lay(g_ffn),
        "wqT": lay(np.asarray(L0_xattn_Wq).T.reshape(H, DH, D)),
        "wkT": lay(np.asarray(L0_xattn_Wk).T.reshape(KV, DH, DV)),
        "wvT": lay(np.asarray(L0_xattn_Wv).T.reshape(KV, DH, DV)),
        "wo": lay(np.asarray(L0_xattn_Wo).reshape(H, DH, D)),
        "gateT": lay(np.asarray(L0_ffn_gate_w).T),
        "rbias": lay(L0_ffn_router_bias),
        "w1": lay(np.concatenate([w1.transpose(1, 0, 2).reshape(D, E * INTER), np.asarray(L0_ffn_sw1).T], 1)),
        "w3": lay(np.concatenate([w3.transpose(1, 0, 2).reshape(D, E * INTER), np.asarray(L0_ffn_sw3).T], 1)),
        "w2": lay(np.concatenate([w2.reshape(E * INTER, D), np.asarray(L0_ffn_sw2).T], 0)),
        "ident": np.eye(128, dtype=np.float32), "pick": pick, "expand": expand, "before": before, "low": low,
    }
    nc = bacc.Bacc("TRN2", target_bir_lowering=False, num_devices=1)
    aps = {n: nc.dram_tensor(f"in_{n}", a.shape, mb.dt.from_np(a.dtype), kind="ExternalInput").ap()
           for n, a in arrays.items()}
    out = nc.dram_tensor("out", (B * T, D), F32, kind="ExternalOutput").ap()
    build(nc, **aps, out=out)
    r = launch(nc, [{f"in_{n}": a for n, a in arrays.items()}], core_ids=[0])
    return r.results[0]["out"].reshape(B, T, D)
```
